# Optimizing a Trainium2 kernel written in Bass

```python
import numpy as np
import jax
import jax.numpy as jnp

def _softmax(x, axis=-1):
    return jax.nn.softmax(x, axis=axis)

def _gelu(x):
    return jax.nn.gelu(x, approximate=True)

def _silu(x):
    return jax.nn.silu(x)

def _sigmoid(x):
    return jax.nn.sigmoid(x)

def _layernorm(x, axis=-1, eps=1e-05):
    m = jnp.mean(x, axis=axis, keepdims=True)
    v = jnp.var(x, axis=axis, keepdims=True)
    return (x - m) / jnp.sqrt(v + eps)

def _scatter_add(tgt, idx, src, axis=0):
    return tgt.at[idx].add(src)

def _segment_sum(src, seg, n):
    return jax.ops.segment_sum(src, seg, n)
kernel_name = 'mk_xattn_seq_d1_seqx_r8_93e95c'

def setup_inputs(seed: int=0):
    np.random.seed(seed)
    _w = jnp.asarray

    def _rec_inputs():
        import jax
        import jax.numpy as jnp
        _rk = jax.random.key(seed)
        x = -0.0002928 + 1 * jax.random.normal(jax.random.fold_in(_rk, 1), (16, 256, 128), jnp.float32)
        _lenS = 256 - jax.random.randint(jax.random.fold_in(_rk, 7), (16,), 0, max(1, 256 // 4) + 1, jnp.int32)
        _lenS2 = 64 - jax.random.randint(jax.random.fold_in(_rk, 8), (16,), 0, max(1, 64 // 4) + 1, jnp.int32)
        _ctx_1024P = jax.random.normal(jax.random.fold_in(_rk, 11), (16, 16, 128), jnp.float32)
        _ctx_1024c = jax.random.dirichlet(jax.random.fold_in(_rk, 511), 0.3 * jnp.ones((16,), jnp.float32), (16, 64))
        _ctx_1024t = jnp.einsum('bsk,bkd->bsd', _ctx_1024c, _ctx_1024P)
        _ctx_1024t = _ctx_1024t * jax.lax.rsqrt(jnp.mean(jnp.square(_ctx_1024t)) + 1e-12) * 0.953939
        ctx_1024 = -1.39393e-06 + 0.999914 * (_ctx_1024t + 0.3 * jax.random.normal(jax.random.fold_in(_rk, 611), (16, 64, 128), jnp.float32))
        _validS = jnp.arange(256)[None, :] < _lenS[:, None]
        _validS2 = jnp.arange(64)[None, :] < _lenS2[:, None]
        _causal = jnp.tril(jnp.ones((256, 256), dtype=bool))
        mask_BxSxS2_bk0 = jnp.logical_not(jnp.broadcast_to(_validS2[:, None, :], (16, 256, 64)))
        return (x, ctx_1024, mask_BxSxS2_bk0)
    x, ctx_1024, mask_BxSxS2_bk0 = _rec_inputs()

    def _L0_xattn_setup():
        import jax, jax.numpy as jnp
        import numpy as np
        EPS = 1e-05

        def layer_norm(x, w, b):
            mu = jnp.mean(x, axis=-1, keepdims=True)
            var = jnp.var(x, axis=-1, keepdims=True)
            return (x - mu) * jax.lax.rsqrt(var + EPS) * w + b
        key = jax.random.key(seed)
        ks = jax.random.split(key, 12)
        B, N, M, C = (2, 256, 256, 128)
        H = 16
        hid = 4 * C
        s = lambda d: 1.0 / np.sqrt(d)
        return {'x': jax.random.normal(ks[0], (B, N, C), jnp.float32), 'context': jax.random.normal(ks[1], (B, M, C), jnp.float32), 'xa_mask': jax.random.bernoulli(ks[2], 0.1, (B, N, M)), 'qn_w': jnp.ones((C,), jnp.float32), 'qn_b': jnp.zeros((C,), jnp.float32), 'cn_w': jnp.ones((C,), jnp.float32), 'cn_b': jnp.zeros((C,), jnp.float32), 'n2_w': jnp.ones((C,), jnp.float32), 'n2_b': jnp.zeros((C,), jnp.float32), 'q_w': jax.random.normal(ks[3], (C, C), jnp.float32) * s(C), 'kv_w': jax.random.normal(ks[4], (C, 2 * C), jnp.float32) * s(C), 'proj_w': jax.random.normal(ks[5], (C, C), jnp.float32) * s(C), 'proj_b': jnp.zeros((C,), jnp.float32), 'fc1_w': jax.random.normal(ks[6], (C, hid), jnp.float32) * s(C), 'fc1_b': jnp.zeros((hid,), jnp.float32), 'fc2_w': jax.random.normal(ks[7], (hid, C), jnp.float32) * s(hid), 'fc2_b': jnp.zeros((C,), jnp.float32)}
    _L0_xattn_all = _L0_xattn_setup()
    _L0_xattn_in = {k: v for k, v in _L0_xattn_all.items() if k in ('qn_w', 'qn_b', 'cn_w', 'cn_b', 'n2_w', 'n2_b', 'q_w', 'kv_w', 'proj_w', 'proj_b', 'fc1_w', 'fc1_b', 'fc2_w', 'fc2_b')}
    del _L0_xattn_all
    return {'x': x, 'ctx_1024': ctx_1024, 'mask_BxSxS2_bk0': mask_BxSxS2_bk0, 'L0_xattn_qn_w': _L0_xattn_in['qn_w'], 'L0_xattn_qn_b': _L0_xattn_in['qn_b'], 'L0_xattn_cn_w': _L0_xattn_in['cn_w'], 'L0_xattn_cn_b': _L0_xattn_in['cn_b'], 'L0_xattn_n2_w': _L0_xattn_in['n2_w'], 'L0_xattn_n2_b': _L0_xattn_in['n2_b'], 'L0_xattn_q_w': _L0_xattn_in['q_w'], 'L0_xattn_kv_w': _L0_xattn_in['kv_w'], 'L0_xattn_proj_w': _L0_xattn_in['proj_w'], 'L0_xattn_proj_b': _L0_xattn_in['proj_b'], 'L0_xattn_fc1_w': _L0_xattn_in['fc1_w'], 'L0_xattn_fc1_b': _L0_xattn_in['fc1_b'], 'L0_xattn_fc2_w': _L0_xattn_in['fc2_w'], 'L0_xattn_fc2_b': _L0_xattn_in['fc2_b']}

def reference(x, ctx_1024, mask_BxSxS2_bk0, L0_xattn_qn_w, L0_xattn_qn_b, L0_xattn_cn_w, L0_xattn_cn_b, L0_xattn_n2_w, L0_xattn_n2_b, L0_xattn_q_w, L0_xattn_kv_w, L0_xattn_proj_w, L0_xattn_proj_b, L0_xattn_fc1_w, L0_xattn_fc1_b, L0_xattn_fc2_w, L0_xattn_fc2_b):
    import jax
    import jax.numpy as jnp

    def _L0_xattn_ref(x, context, xa_mask, qn_w, qn_b, cn_w, cn_b, n2_w, n2_b, q_w, kv_w, proj_w, proj_b, fc1_w, fc1_b, fc2_w, fc2_b):
        import jax, jax.numpy as jnp
        import numpy as np
        EPS = 1e-05

        def layer_norm(x, w, b):
            mu = jnp.mean(x, axis=-1, keepdims=True)
            var = jnp.var(x, axis=-1, keepdims=True)
            return (x - mu) * jax.lax.rsqrt(var + EPS) * w + b
        B, N, C = x.shape
        M = context.shape[1]
        H = 16
        D = C // H
        scale = D ** (-0.5)
        xq = layer_norm(x, qn_w, qn_b)
        ctx = layer_norm(context, cn_w, cn_b)
        q = (xq @ q_w).reshape(B, N, H, D)
        kv = (ctx @ kv_w).reshape(B, M, 2, H, D)
        k, v = (kv[:, :, 0], kv[:, :, 1])
        attn = jnp.einsum('bnhd,bmhd->bhnm', q, k) * scale
        neg = -jnp.finfo(attn.dtype).max
        attn = jnp.where(xa_mask[:, None, :, :], neg, attn)
        attn = jax.nn.softmax(attn, axis=-1)
        out = jnp.einsum('bhnm,bmhd->bnhd', attn, v).reshape(B, N, C)
        out = out @ proj_w + proj_b
        x = x + out
        h = layer_norm(x, n2_w, n2_b)
        h = jax.nn.gelu(h @ fc1_w + fc1_b, approximate=False) @ fc2_w + fc2_b
        return x + h
    x = _L0_xattn_ref(x, ctx_1024, mask_BxSxS2_bk0, L0_xattn_qn_w, L0_xattn_qn_b, L0_xattn_cn_w, L0_xattn_cn_b, L0_xattn_n2_w, L0_xattn_n2_b, L0_xattn_q_w, L0_xattn_kv_w, L0_xattn_proj_w, L0_xattn_proj_b, L0_xattn_fc1_w, L0_xattn_fc1_b, L0_xattn_fc2_w, L0_xattn_fc2_b)
    return x

_drawn_inputs = setup_inputs


def setup_inputs(seed=0):
    import zlib

    import numpy as np

    out = dict(_drawn_inputs(seed))
    spreads = {'L0_xattn_qn_w': (1.0, 0.2),
     'L0_xattn_qn_b': (0.0, 0.407),
     'L0_xattn_cn_w': (1.0, 0.2),
     'L0_xattn_cn_b': (0.0, 0.1),
     'L0_xattn_n2_w': (1.0, 0.2),
     'L0_xattn_n2_b': (0.0, 0.1),
     'L0_xattn_proj_b': (0.0, 0.1),
     'L0_xattn_fc1_b': (0.0, 0.1),
     'L0_xattn_fc2_b': (0.0, 0.1)}
    factors = {}
    for name, (base, spread) in spreads.items():
        noise = np.random.default_rng([zlib.crc32(name.encode()), seed]).standard_normal(out[name].shape)
        drawn = base * np.exp(spread * noise) if base else spread * noise
        out[name] = jnp.asarray(drawn.astype(out[name].dtype))
    for name, factor in factors.items():
        out[name] = (out[name] * factor).astype(out[name].dtype)
    return out
```

```python
from contextlib import ExitStack

import numpy as np

import concourse.bass as bass
from concourse import mybir

F32 = mybir.dt.float32
F32R = mybir.dt.float32r
BF16 = mybir.dt.bfloat16
ALU = mybir.AluOpType
ACT = mybir.ActivationFunctionType
AX = mybir.AxisListType

P = 128
B, N, M, C = 16, 256, 64, 128
H = 16
D = C // H
HID = 4 * C
EPS = 1e-5
SCALE = float(D) ** -0.5
BIG = float(2.0 ** 96)
G = 4
HG = H // G
R = HG * D
TB = N // P
NT = B * TB
NC = B * M // P
NPAIR = H // 2
MC = M + 2 * H
KH = HID // P
CH = 4
NCH = NT // CH
WQ, WK, WV, WP, W1, W2 = 0, C, 2 * C, 3 * C, 4 * C, 4 * C + HID
WCOLS = W2 + HID


def ds(start, size):
    return bass.ds(start, size)


def xattn_block(nc, x, ctx_in, mask, weights, vecs, rows, ident_in, identb_in, hsel_in, vsel_in,
                rsel_in, out):
    stack = ExitStack()
    with stack:
        def sb(name, shape, dt):
            return stack.enter_context(nc.sbuf_tensor(name, shape, dt))

        def sem(name):
            return stack.enter_context(nc.semaphore(name))

        bank = [stack.enter_context(nc.psum_tensor(f"bank{n}", [P, 512], F32)) for n in range(8)]

        w = sb("w", [P, WCOLS], F32)
        vec = sb("vec", [P, 6 + KH], F32)
        row = sb("row", [P, 2, C], F32)
        ident = sb("ident", [P, P], F32)
        identb = sb("identb", [P, P], BF16)
        hsel = sb("hsel", [P, HG], F32)
        vsel = sb("vsel", [P, 2, R], F32)
        rsel = sb("rsel", [MC, NPAIR, P], BF16)
        xs = sb("xs", [P, NT, C], F32)
        x1 = sb("x1", [P, NT, C], F32)
        wq = sb("wq", [P, C], F32)
        wk = sb("wk", [P, C], F32)
        wv = sb("wv", [P, C], F32)
        w1 = sb("w1", [P, HID], F32)
        w1hl = sb("w1hl", [P, 2, HID], F32R)
        b1 = sb("b1", [P, KH], F32)
        pb = sb("pb", [P, C], F32)
        fold = sb("fold", [P, 2, P], F32)
        fcol = sb("fcol", [P, 3], F32)
        ones = sb("ones", [P, P], F32)
        cs = sb("cs", [P, NC, C], F32)
        cn = sb("cn", [P, NC, C], F32)
        ct = sb("ct", [P, B, 2, M], F32)
        khl = sb("khl", [P, 2, B * M], F32R)
        ks = sb("ks", [P, G, B * M], F32R)
        vraw = sb("vraw", [P, B, C], F32)
        mkw = sb("mkw", [P, NT, M // 4], mybir.dt.int32)
        mk = mkw[:, :, :].bitcast(mybir.dt.uint8)
        maskbig = sb("maskbig", [P, NT, M], BF16)
        effm = sb("effm", [P, NT, M], BF16)
        allm = sb("allm", [P, NT], F32)
        NS = NC + NT
        stats = sb("stats", [P, NS, 6], F32)
        sa = sb("sa", [P, NS], F32)
        sd = sb("sd", [P, NS], F32)
        sq = sb("sq", [P, NS], F32)
        mean = sb("mean", [P, NS], F32)
        var = sb("var", [P, NS], F32)
        std = sb("std", [P, NS], F32)
        rstd = sb("rstd", [P, NS], F32)
        shift = sb("shift", [P, NS], F32)
        ln_done, nr_done, dr_done = sem("ln_done"), sem("nr_done"), sem("dr_done")
        stats2 = sb("stats2", [P, NT, 6], F32)
        xn = [sb(f"xn{p}", [P, TB, C], F32) for p in range(2)]
        xt = sb("xt", [P, N], F32)
        qhl = [sb(f"qhl{p}", [P, 2, N], F32R) for p in range(2)]
        qs = [sb(f"qs{p}", [P, G, N], F32R) for p in range(4)]
        kbd = [sb(f"kbd{p}", [P, G, HG, M], F32R) for p in range(2)]
        vbd = [sb(f"vbd{p}", [P, G, 2, R], F32) for p in range(2)]
        mc = [sb(f"mc{p}", [P, TB, MC], BF16) for p in range(2)]
        cmax = sb("cmax", [P, TB, H], F32)
        mct = [sb(f"mct{p}", [MC, N], BF16) for p in range(2)]
        pt = [sb(f"pt{p}", [P, NPAIR, N], F32) for p in range(2)]
        lnd = sb("lnd", [P, N], F32)
        rden = sb("rden", [P, N], F32)
        nr = sb("nr", [P, N], F32)
        dr = sb("dr", [P, N], F32)
        on = [sb(f"on{p}", [P, N], F32) for p in range(2)]
        h2 = [sb(f"h2{p}", [P, CH, C], F32) for p in range(2)]
        hhl = [sb(f"hhl{p}", [P, 2, CH * P], F32R) for p in range(2)]
        gl = [sb(f"gl{p}", [P, KH, CH * P], F32) for p in range(2)]
        x1b = [sb(f"x1b{p}", [P, CH, C], F32) for p in range(2)]
        yo = [sb(f"yo{p}", [P, CH, C], F32) for p in range(2)]

        s_bank = bank[0:4]
        t_bank = bank[4:6]
        od = bank[6]
        misc = bank[7]

        ld_w, ld_v, ld_c, ld_m = sem("ld_w"), sem("ld_v"), sem("ld_c"), sem("ld_m")
        ld_x = [sem(f"ld_x{n}") for n in range(4)]
        dve = sem("dve_chain")
        wfold_in, qfold_mm, wready, bfold_mm, bv_copied, pb_mm = (
            sem("wfold_in"), sem("qfold_mm"), sem("wready"), sem("bfold_mm"), sem("bv_copied"), sem("pb_mm"))
        var_ready, std_ready, scales_ready = sem("var_ready"), sem("std_ready"), sem("scales_ready")
        cn_ready, ct_tr, ct_ready, k_mm, k_hi, k_split, ks_loaded = (
            sem("cn_ready"), sem("ct_tr"), sem("ct_ready"), sem("k_mm"), sem("k_hi"), sem("k_split"),
            sem("ks_loaded"))
        v_mm, v_ready, mask_ready, pb_ready = sem("v_mm"), sem("v_ready"), sem("mask_ready"), sem("pb_ready")
        xn_done, xt_tr, xt_done, q_mm, qhi_done, qlo_done = (
            sem("xn_done"), sem("xt_tr"), sem("xt_done"), sem("q_mm"), sem("qhi_done"), sem("qlo_done"))
        qs_loaded = [sem(f"qs_loaded{p}") for p in range(4)]
        kbd_done, vbd_done, mcm_done, xb_done = sem("kbd_done"), sem("vbd_done"), sem("mcm_done"), sem("xb_done")
        s_mm, s_red, chi_done, clo_done, mct_tr, mct_done = (
            sem("s_mm"), sem("s_red"), sem("chi_done"), sem("clo_done"), sem("mct_tr"), sem("mct_done"))
        t_mm, exp_done, od_mm, rden_done, on_done, pj_mm, x1_done, st2_done = (
            sem("t_mm"), sem("exp_done"), sem("od_mm"), sem("rden_done"), sem("on_done"), sem("pj_mm"),
            sem("x1_done"), sem("st2_done"))
        var2_ready, std2_ready, h2_done, h2_tr, hhi_done, hlo_done, f1_mm, gelu_done, y_mm, y_done = (
            sem("var2_ready"), sem("std2_ready"), sem("h2_done"), sem("h2_tr"), sem("hhi_done"),
            sem("hlo_done"), sem("f1_mm"), sem("gelu_done"), sem("y_mm"), sem("y_done"))
        x1b_done = sem("x1b_done")
        yo_free = [sem("yo_free0"), sem("yo_free1")]

        block = stack.enter_context(nc.Block())

        def has(b):
            return not isinstance(b, int) or 0 <= b < B

        def hasc(j):
            return not isinstance(j, int) or 0 <= j < NCH

        def wait(eng, s, value):
            if not isinstance(value, int) or value > 0:
                eng.wait_ge(s, value)

        def value(eng, v):
            return v if isinstance(v, int) else eng.snap(v)

        def steps(eng, step):
            for i in range(2):
                step(i, i)
            with eng.Fori(0, (B - 4) // 4) as t:
                for e in range(2, 6):
                    step(4 * t + e, e % 4)
            for i in range(B - 2, B + 2):
                step(i, i % 4)

        def copied_slots(b, turn):
            return 16 * (b - turn) + 64

        def chunk_steps(eng, step):
            for j in range(2):
                step(j, j)
            with eng.Fori(0, 2) as t:
                step(2 * t + 2, 0)
                step(2 * t + 3, 1)
            for j in range(6, NCH + 1):
                step(j, j % 2)

        @block.sync
        def _(sp):
            for par in range(2):
                sp.sem_inc(yo_free[par], 16)
            sp.dma_start(cs[:, :, :], ctx_in.rearrange("(u e) m c -> (e m) u c", e=2)).then_inc(ld_c, 16)
            sp.dma_start(w[:, :], weights).then_inc(ld_w, 16)
            sp.dma_start(vec[:, :], vecs).then_inc(ld_v, 16)
            sp.dma_start(ident[:, :], ident_in).then_inc(ld_v, 16)
            xv = x.rearrange("b (t p) c -> p (b t) c", p=P)
            for n in range(4):
                sp.dma_start(xs[:, 8 * n:8 * n + 8, :], xv[:, 8 * n:8 * n + 8, :]).then_inc(ld_x[n], 16)
            sp.wait_ge(k_split, 2)
            for s in range(4):
                sp.dma_start(ks[R * s:R * s + R, :, :].bitcast(F32), khl[:, s % 2, :].bitcast(F32))\
                  .then_inc(ks_loaded, 16)

            def slots(b, turn):
                for part, done in enumerate((qhi_done, qlo_done)):
                    sp.wait_ge(done, b + 1)
                    for s in range(2):
                        at = R * (2 * part + s)
                        sp.dma_start(qs[turn][at:at + R, :, :].bitcast(F32), qhl[turn % 2][:, part, :].bitcast(F32))\
                          .then_inc(qs_loaded[turn], 16)

            with sp.Fori(0, B // 4) as t:
                for e in range(4):
                    slots(4 * t + e, e)

            ov = out.rearrange("b (t p) c -> p (b t) c", p=P)

            def store(j, par):
                first, ready = value(sp, CH * j), value(sp, j + 1)
                sp.wait_ge(y_done, ready)
                sp.dma_start(ov[:, ds(first, CH), :], yo[par][:, :, :]).then_inc(yo_free[par], 16)

            with sp.Fori(0, NCH // 2) as t:
                store(2 * t, 0)
                store(2 * t + 1, 1)
            for par in range(2):
                sp.wait_ge(yo_free[par], 16 * (NCH // 2) + 16)

        @block.gpsimd
        def _(pool):
            pool.dma_start(mkw[:, :, :], mask).then_inc(ld_m, 16)
            pool.dma_start(identb[:, :].bitcast(mybir.dt.uint16), identb_in).then_inc(ld_m, 16)
            pool.dma_start(row[:, :, :], rows.partition_broadcast(P)).then_inc(ld_m, 16)
            pool.dma_start(hsel[:, :], hsel_in).then_inc(ld_m, 16)
            pool.dma_start(vsel[:, :, :], vsel_in).then_inc(ld_m, 16)
            pool.dma_start(rsel[:, :, :].bitcast(mybir.dt.uint16), rsel_in).then_inc(ld_m, 16)
            pool.wait_ge(ld_m, 96)

            def prepare(b, par):
                wait(pool, mct_tr, b - 1)
                nc.gpsimd.tensor_copy(mc[par][:, :, 0:M], maskbig[:, ds(TB * b, TB), :]).then_inc(mcm_done, 1)
                wait(pool, t_mm, 4 * (b - 1))
                nc.gpsimd.tensor_tensor(
                    kbd[par][:, :, :, :],
                    ks[:, :, ds(M * b, M)].bitcast(F32).unsqueeze(2).to_broadcast([P, G, HG, M]),
                    hsel[:, :].unsqueeze(1).unsqueeze(3).to_broadcast([P, G, HG, M]), ALU.mult)\
                    .then_inc(kbd_done, 1)
                nc.gpsimd.tensor_tensor(
                    x1[:, ds(TB * b, TB), :], xs[:, ds(TB * b, TB), :],
                    pb[:, :].unsqueeze(1).to_broadcast([P, TB, C]), ALU.add).then_inc(xb_done, 1)

            def prepare_v(b, par):
                wait(pool, od_mm, b - 1)
                nc.gpsimd.tensor_tensor(
                    vbd[par][:, :, :, :],
                    vraw[:, ds(b, 1), :].rearrange("p o (q r) -> p (o q) r", q=G).unsqueeze(2)
                    .to_broadcast([P, G, 2, R]),
                    vsel[:, :, :].unsqueeze(1).to_broadcast([P, G, 2, R]), ALU.mult).then_inc(vbd_done, 1)

            pool.wait_ge(ks_loaded, 64)
            pool.wait_ge(mask_ready, 1)
            pool.wait_ge(v_ready, 4)
            pool.wait_ge(pb_ready, 1)
            for n in range(4):
                pool.wait_ge(ld_x[n], 16)
            prepare(0, 0)
            prepare(1, 1)
            prepare_v(0, 0)
            prepare(2, 0)
            prepare_v(1, 1)
            with pool.Fori(0, (B - 4) // 2) as t:
                prepare(2 * t + 3, 1)
                prepare_v(2 * t + 2, 0)
                prepare(2 * t + 4, 0)
                prepare_v(2 * t + 3, 1)
            prepare(B - 1, 1)
            prepare_v(B - 2, 0)
            prepare_v(B - 1, 1)

            def residual(j, par):
                pool.wait_ge(x1_done, B)
                wait(pool, y_done, j - 1)
                nc.gpsimd.tensor_tensor(
                    x1b[par][:, :, :], x1[:, ds(CH * j, CH), :],
                    row[:, 1:2, :].to_broadcast([P, CH, C]), ALU.add).then_inc(x1b_done, 1)

            residual(0, 0)
            residual(1, 1)
            with pool.Fori(0, NCH // 2 - 1) as t:
                residual(2 * t + 2, 0)
                residual(2 * t + 3, 1)

        @block.scalar
        def _(act):
            act.wait_ge(var_ready, 1)
            nc.scalar.activation(std[:, :], var[:, :], ACT.Sqrt).then_inc(std_ready, 1)
            nc.scalar.preload_act_table_set("natural_log_exp_and_others")
            for n in range(2):
                act.wait_ge(ct_tr, n + 1)
                for e in range(2):
                    last = nc.scalar.activation(ct[:, 8 * n:8 * n + 8, e, :],
                                                s_bank[n][:, :].rearrange("p (b m) -> p b m", m=M), ACT.Copy)
                last.then_inc(ct_ready, 1)
            for n in range(2):
                act.wait_ge(k_mm, n + 1)
                act.wait_ge(wready, 4)
                nc.scalar.activation(khl[:, 0, 512 * n:512 * n + 512], s_bank[2 + n][:, :], ACT.Identity,
                                     bias=fcol[:, 1:2]).then_inc(k_hi, 1)
            act.wait_ge(scales_ready, 1)

            def normalise(b, par):
                wait(act, xt_tr, b - 1)
                for t in range(TB):
                    last = nc.scalar.activation(
                        xn[par][:, t, :], xs[:, ds(TB * b + t, 1), :].squeeze(1), ACT.Identity,
                        bias=shift[:, ds(NC + TB * b + t, 1)], scale=rstd[:, ds(NC + TB * b + t, 1)])
                last.then_inc(xn_done, 1)

            def x_copied(b):
                act.wait_ge(xt_tr, b + 1)
                nc.scalar.activation(xt[:, :], misc[:, 0:N], ACT.Copy).then_inc(xt_done, 1)

            def q_high(b, turn):
                act.wait_ge(q_mm, b + 1)
                if not isinstance(b, int) or b >= 2:
                    before = (turn + 2) % 4
                    act.wait_ge(qs_loaded[before], copied_slots(b - 2, before))
                nc.scalar.activation(qhl[turn % 2][:, 0, :], misc[:, 0:N], ACT.Copy).then_inc(qhi_done, 1)

            def inverse(b):
                act.wait_ge(od_mm, b + 1)
                nc.scalar.activation(lnd[:, :], od[:, N:2 * N], ACT.Ln).then_inc(ln_done, 1)
                act.wait_ge(ln_done, b + 1)
                nc.scalar.activation(rden[:, :], lnd[:, :], ACT.Exp, scale=-1.0).then_inc(rden_done, 1)

            def mct_copied(b, par):
                act.wait_ge(mct_tr, b + 1)
                nc.scalar.activation(mct[par][:, :], misc[0:MC, 0:N // 2].bitcast(BF16), ACT.Copy)\
                    .then_inc(mct_done, 1)

            for b in range(2):
                normalise(b, b)
                x_copied(b)
                q_high(b, b)
            for n in range(4):
                act.wait_ge(v_mm, n + 1)
                nc.scalar.activation(vraw[:, 4 * n:4 * n + 4, :], s_bank[n][:, :].rearrange("p (b c) -> p b c", c=C),
                                     ACT.Copy).then_inc(v_ready, 1)
            mct_copied(0, 0)

            def exps(b, k, par):
                if k == 0:
                    wait(act, od_mm, b - 1)
                act.wait_ge(t_mm, 4 * b + k + 1)
                nc.scalar.activation(pt[par][:, 2 * k:2 * k + 2, :],
                                     t_bank[k % 2][:, :].rearrange("p (j n) -> p j n", j=2),
                                     ACT.Exp, scale=SCALE).then_inc(exp_done, 1)

            def step(i, turn):
                par = turn % 2
                if has(i + 2):
                    normalise(i + 2, par)
                for k in range(4):
                    if has(i):
                        exps(i, k, par)
                    if k == 1 and has(i + 2):
                        x_copied(i + 2)
                    if k == 2 and has(i + 2):
                        q_high(i + 2, (turn + 2) % 4)
                if has(i + 1):
                    mct_copied(i + 1, 1 - par)
                if has(i - 1):
                    inverse(i - 1)

            steps(act, step)

            act.wait_ge(var2_ready, 1)
            nc.scalar.activation(std[:, 0:NT], var[:, 0:NT], ACT.Sqrt).then_inc(std2_ready, 1)

            def h_high(j, par):
                act.wait_ge(h2_tr, j + 1)
                wait(act, f1_mm, KH * (j - 1))
                nc.scalar.activation(hhl[par][:, 0, :], od[:, :], ACT.Copy).then_inc(hhi_done, 1)

            h_high(0, 0)

            def mlp(j, par):
                for k in range(KH):
                    if hasc(j):
                        if k == 0:
                            wait(act, y_mm, j - 1)
                        act.wait_ge(f1_mm, KH * j + k + 1)
                        nc.scalar.activation(gl[par][:, k, :], s_bank[k][:, :], ACT.Gelu, bias=b1[:, k:k + 1])\
                            .then_inc(gelu_done, 1)
                    if k == 1 and hasc(j + 1):
                        h_high(j + 1, 1 - par)

            chunk_steps(act, mlp)

        @block.vector
        def _(v):
            chain = [0]

            def link(ins):
                chain[0] += 1
                ins.then_inc(dve, 1)
                v.wait_ge(dve, chain[0])

            def variance(st, n, ready):
                nc.vector.tensor_tensor(sa[:, 0:n], st[:, 0:n, 2], st[:, 0:n, 5], ALU.add)
                nc.vector.tensor_tensor(mean[:, 0:n], st[:, 0:n, 1], st[:, 0:n, 4], ALU.add)
                link(nc.vector.tensor_tensor(sd[:, 0:n], st[:, 0:n, 1], st[:, 0:n, 4], ALU.subtract))
                nc.vector.tensor_scalar(mean[:, 0:n], mean[:, 0:n], 0.5, None, ALU.mult)
                nc.vector.tensor_scalar(sa[:, 0:n], sa[:, 0:n], 1.0 / C, EPS, ALU.mult, ALU.add)
                link(nc.vector.scalar_tensor_tensor(sq[:, 0:n], sd[:, 0:n], 0.25, sd[:, 0:n], ALU.mult, ALU.mult))
                nc.vector.tensor_tensor(var[:, 0:n], sq[:, 0:n], sa[:, 0:n], ALU.add).then_inc(ready, 1)

            nc.vector.memset(ones[:, :], 1.0)
            v.wait_ge(ld_c, 16)
            for u in range(NC):
                nc.vector.bn_stats(stats[:, u, :], cs[:, u, :])
            for t in range(NT):
                if t % 8 == 0:
                    v.wait_ge(ld_x[t // 8], 16)
                last = nc.vector.bn_stats(stats[:, NC + t, :], xs[:, t, :])
            link(last)
            variance(stats, NS, var_ready)
            v.wait_ge(ld_w, 16)
            v.wait_ge(ld_v, 32)
            link(nc.vector.tensor_tensor(fcol[:, 0:1], vec[:, 1:2], vec[:, 0:1], ALU.subtract))
            nc.vector.tensor_scalar(fold[:, 0, :], ones[:, :], fcol[:, 0:1], 1.0 / C, ALU.mult, ALU.mult)\
                .then_inc(wfold_in, 1)
            nc.vector.tensor_scalar(wk[:, :], w[:, WK:WK + C], vec[:, 2:3], None, ALU.mult).then_inc(wready, 1)
            nc.vector.tensor_scalar(wv[:, :], w[:, WV:WV + C], vec[:, 2:3], None, ALU.mult).then_inc(wready, 1)
            v.wait_ge(ld_m, 96)
            link(nc.vector.tensor_reduce(allm[:, :], mk[:, :, :], AX.X, ALU.min))
            link(nc.vector.tensor_tensor(effm[:, :, :], allm[:, :].unsqueeze(2).to_broadcast([P, NT, M]),
                                         mk[:, :, :], ALU.subtract))
            nc.vector.tensor_scalar(maskbig[:, :, :], effm[:, :, :], BIG, None, ALU.mult).then_inc(mask_ready, 1)
            link(nc.vector.tensor_scalar(allm[:, :], allm[:, :], -1.0, 1.0, ALU.mult, ALU.add))
            v.wait_ge(std_ready, 1)
            link(nc.vector.reciprocal(rstd[:, :], std[:, :]))
            for u in range(NC):
                last = nc.vector.tensor_scalar(cn[:, u, :], cs[:, u, :], mean[:, u:u + 1], rstd[:, u:u + 1],
                                               ALU.subtract, ALU.mult)
                if u % 4 == 3:
                    last.then_inc(cn_ready, 1)
            link(nc.vector.tensor_tensor(rstd[:, NC:NS], rstd[:, NC:NS], allm[:, :], ALU.mult))
            nc.vector.tensor_tensor(shift[:, NC:NS], mean[:, NC:NS], rstd[:, NC:NS], ALU.mult)
            link(nc.vector.memset(sq[:, 0:1], 0.0))
            nc.vector.tensor_tensor(shift[:, NC:NS], allm[:, :], shift[:, NC:NS], ALU.subtract)\
                .then_inc(scales_ready, 1)
            v.wait_ge(qfold_mm, 1)
            nc.vector.scalar_tensor_tensor(wq[:, :], w[:, WQ:WQ + C], vec[:, 0:1], misc[:, 0:C],
                                           ALU.mult, ALU.add).then_inc(wready, 1)
            v.wait_ge(bfold_mm, 1)
            nc.vector.tensor_tensor(b1[:, :], od[:, 2:2 + KH], vec[:, 6:6 + KH], ALU.add)
            nc.vector.tensor_scalar(fold[:, 1, :], ones[:, :], od[:, 1:2], None, ALU.mult).then_inc(bv_copied, 1)
            nc.vector.tensor_copy(fcol[:, 1:2], od[:, 0:1]).then_inc(wready, 1)
            v.wait_ge(pb_mm, 1)
            nc.vector.tensor_tensor(pb[:, :], misc[:, 128:128 + C], row[:, 0, :], ALU.add).then_inc(pb_ready, 1)
            for n in range(2):
                v.wait_ge(k_hi, n + 1)
                nc.vector.scalar_tensor_tensor(
                    khl[:, 1, 512 * n:512 * n + 512], s_bank[2 + n][:, :], fcol[:, 1:2],
                    khl[:, 0, 512 * n:512 * n + 512].bitcast(F32), ALU.add, ALU.subtract).then_inc(k_split, 1)

            def q_low(b, par):
                v.wait_ge(qhi_done, b + 1)
                nc.vector.tensor_tensor(qhl[par][:, 1, :], misc[:, 0:N], qhl[par][:, 0, :].bitcast(F32),
                                        ALU.subtract).then_inc(qlo_done, 1)

            def maxima(b, k):
                t, half = k // 2, k % 2
                v.wait_ge(s_mm, 4 * b + k + 1)
                nc.vector.tensor_reduce(cmax[:, t, 8 * half:8 * half + 8],
                                        s_bank[k][:, :].rearrange("p (h m) -> p h m", m=M), AX.X, ALU.max)\
                    .then_inc(s_red, 1)

            def max_parts(b, par):
                v.wait_ge(s_red, 4 * b + 4)
                wait(v, mct_tr, b - 1)
                nc.vector.tensor_scalar(mc[par][:, :, M:M + H], cmax[:, :, :], -1.0, None, ALU.mult)\
                    .then_inc(chi_done, 1)
                v.wait_ge(chi_done, b + 1)
                nc.vector.scalar_tensor_tensor(mc[par][:, :, M + H:MC], cmax[:, :, :], -1.0,
                                               mc[par][:, :, M:M + H], ALU.mult, ALU.subtract)\
                    .then_inc(clo_done, 1)

            def add_residual(b):
                v.wait_ge(pj_mm, b + 1)
                v.wait_ge(xb_done, b + 1)
                nc.vector.tensor_tensor(x1[:, ds(TB * b, TB), :], x1[:, ds(TB * b, TB), :],
                                        misc[:, 0:N].rearrange("p (t c) -> p t c", t=TB),
                                        ALU.subtract).then_inc(x1_done, 1)

            def quotient(b, par):
                v.wait_ge(rden_done, b + 1)
                nc.vector.tensor_tensor(nr[:, :], od[:, 0:N], rden[:, :], ALU.mult).then_inc(nr_done, 1)
                nc.vector.tensor_tensor(dr[:, :], od[:, N:2 * N], rden[:, :], ALU.mult).then_inc(dr_done, 1)
                v.wait_ge(nr_done, b + 1)
                v.wait_ge(dr_done, b + 1)
                nc.vector.scalar_tensor_tensor(on[par][:, :], dr[:, :], 2.0, nr[:, :], ALU.subtract, ALU.mult)\
                    .then_inc(on_done, 1)

            def row_stats(b):
                v.wait_ge(x1_done, b + 1)
                for t in range(TB):
                    last = nc.vector.bn_stats(stats2[:, ds(TB * b + t, 1), :].squeeze(1),
                                              x1[:, ds(TB * b + t, 1), :].squeeze(1))
                last.then_inc(st2_done, 1)

            q_low(0, 0)
            q_low(1, 1)
            for k in range(4):
                maxima(0, k)
            max_parts(0, 0)

            def step(i, turn):
                par = turn % 2
                for k in range(4):
                    if has(i + 1):
                        maxima(i + 1, k)
                    if k == 2 and has(i + 2):
                        q_low(i + 2, par)
                if has(i + 1):
                    max_parts(i + 1, 1 - par)
                if has(i - 2):
                    add_residual(i - 2)
                if has(i - 1):
                    quotient(i - 1, 1 - par)
                if has(i - 2):
                    row_stats(i - 2)

            steps(v, step)

            v.wait_ge(st2_done, B)
            variance(stats2, NT, var2_ready)
            v.wait_ge(std2_ready, 1)
            link(nc.vector.reciprocal(rstd[:, 0:NT], std[:, 0:NT]))

            def normalise(j, par):
                wait(v, h2_tr, j - 1)
                for t in range(CH):
                    last = nc.vector.tensor_scalar(
                        h2[par][:, t, :], x1[:, ds(CH * j + t, 1), :].squeeze(1), mean[:, ds(CH * j + t, 1)],
                        rstd[:, ds(CH * j + t, 1)], ALU.subtract, ALU.mult)
                last.then_inc(h2_done, 1)

            def h_low(j, par):
                v.wait_ge(hhi_done, j + 1)
                nc.vector.tensor_tensor(hhl[par][:, 1, :], od[:, :], hhl[par][:, 0, :].bitcast(F32),
                                        ALU.subtract).then_inc(hlo_done, 1)

            def result(j, par):
                v.wait_ge(y_mm, j + 1)
                v.wait_ge(x1b_done, j + 1)
                v.wait_ge(yo_free[par], 16 * (j // 2 + 1) if isinstance(j, int) else 8 * (j - par) + 16)
                nc.vector.tensor_tensor(yo[par][:, :, :], t_bank[par][:, :].rearrange("p (t c) -> p t c", t=CH),
                                        x1b[par][:, :, :], ALU.add).then_inc(y_done, 1)

            normalise(0, 0)
            link(nc.vector.tensor_scalar(w1[:, :], w[:, W1:W1 + HID], vec[:, 4:5], None, ALU.mult))
            link(nc.vector.tensor_copy(w1hl[:, 0, :], w1[:, :]))
            nc.vector.tensor_tensor(w1hl[:, 1, :], w1[:, :], w1hl[:, 0, :].bitcast(F32), ALU.subtract)
            h_low(0, 0)
            normalise(1, 1)

            def mlp(j, par):
                if hasc(j + 1):
                    h_low(j + 1, 1 - par)
                if hasc(j + 2):
                    normalise(j + 2, par)
                if hasc(j - 1):
                    result(j - 1, 1 - par)

            chunk_steps(v, mlp)

        @block.tensor
        def _(pe):
            def mm(o, lhsT, rhs, start, stop, **kw):
                return nc.tensor.matmul(o, lhsT, rhs, start=start, stop=stop, **kw)

            pe.wait_ge(ld_w, 16)
            pe.wait_ge(ld_v, 32)
            mm(od[:, 0:1], w[:, WK:WK + C], vec[:, 3:4], True, True)
            mm(od[:, 1:2], w[:, WV:WV + C], vec[:, 3:4], True, True)
            for k in range(KH):
                last = mm(od[:, 2 + k:3 + k], w[:, W1 + P * k:W1 + P * k + P], vec[:, 5:6], True, True)
            last.then_inc(bfold_mm, 1)
            pe.wait_ge(wfold_in, 1)
            mm(misc[:, 0:C], fold[:, 0, :], w[:, WQ:WQ + C], True, True).then_inc(qfold_mm, 1)
            for n in range(2):
                pe.wait_ge(cn_ready, n + 1)
                for u in range(4):
                    last = nc.tensor.transpose(s_bank[n][:, P * u:P * u + P], cn[:, 4 * n + u, :], ident[:, :])
                last.then_inc(ct_tr, 1)
            pe.wait_ge(wready, 2)
            for n in range(2):
                pe.wait_ge(ct_ready, n + 1)
                mm(s_bank[2 + n][:, :], wk[:, :], ct[:, 8 * n:8 * n + 8, 0, :], True, True).then_inc(k_mm, 1)
            pe.wait_ge(bv_copied, 1)
            mm(misc[:, 128:128 + C], fold[:, 1, :], w[:, WP:WP + C], True, True).then_inc(pb_mm, 1)
            pe.wait_ge(pb_ready, 1)

            def x_transposed(b, par):
                pe.wait_ge(xn_done, b + 1)
                for t in range(TB):
                    last = nc.tensor.transpose(misc[:, P * t:P * t + P], xn[par][:, t, :], ident[:, :])
                last.then_inc(xt_tr, 1)

            def project_q(b):
                pe.wait_ge(xt_done, b + 1)
                mm(misc[:, 0:N], wq[:, :], xt[:, :], True, True).then_inc(q_mm, 1)

            def scores_for_max(b, k, turn):
                t, half, par = k // 2, k % 2, turn % 2
                if k == 0:
                    pe.wait_ge(kbd_done, b + 1)
                    pe.wait_ge(mcm_done, b + 1)
                    pe.wait_ge(qs_loaded[turn], copied_slots(b, turn))
                wait(pe, s_red, 4 * (b - 1) + k + 1)
                mm(s_bank[k][:, :], identb[:, :], mc[par][:, t, 0:M].unsqueeze(1).to_broadcast([P, 8, M]),
                   True, False)
                for e in range(2):
                    g = 2 * half + e
                    last = mm(s_bank[k][:, 256 * e:256 * e + 256], qs[turn][:, g, P * t:P * t + P],
                              kbd[par][:, g, :, :], False, e == 1)
                last.then_inc(s_mm, 1)

            def max_transposed(b, par):
                pe.wait_ge(clo_done, b + 1)
                for t in range(TB):
                    last = nc.tensor.transpose(misc[0:MC, 64 * t:64 * t + 64].bitcast(BF16), mc[par][:, t, :],
                                               identb[:, :])
                last.then_inc(mct_tr, 1)

            def scores(b, k, turn):
                par = turn % 2
                if k == 0:
                    pe.wait_ge(mct_done, b + 1)
                wait(pe, exp_done, 4 * b + k - 1)
                for a in range(2):
                    o = t_bank[k % 2][:, N * a:N * a + N]
                    mm(o, kbd[par][:, k, 2 * a:2 * a + 2, :], qs[turn][:, k, :], True, False)
                    last = mm(o, rsel[:, 2 * k + a, :], mct[par][:, :], False, True)
                last.then_inc(t_mm, 1)

            def weighted(par, lhs, off, a):
                for q in range(G):
                    last = mm(od[R * q:R * q + R, off:off + N], lhs(q, a), pt[par][:, 2 * q + a, :],
                              a == 0, a == 1, tile_position=(0, R * q))
                return last

            def numerator(b, par):
                pe.wait_ge(exp_done, 4 * b + 4)
                pe.wait_ge(vbd_done, b + 1)
                wait(pe, on_done, b)
                for a in range(2):
                    weighted(par, lambda q, a: vbd[par][:, q, a, :], 0, a)

            def denominator(b, par, a):
                last = weighted(par, lambda q, a: vsel[:, a, :], N, a)
                if a == 1:
                    last.then_inc(od_mm, 1)

            def project(b, par):
                pe.wait_ge(on_done, b + 1)
                for t in range(TB):
                    last = mm(misc[:, P * t:P * t + P], on[par][:, P * t:P * t + P], w[:, WP:WP + C], True, True)
                last.then_inc(pj_mm, 1)

            pe.wait_ge(wready, 4)
            for b in range(2):
                x_transposed(b, b)
                project_q(b)
                pe.wait_ge(qlo_done, b + 1)
            for n in range(4):
                if n < 2:
                    pe.wait_ge(ct_ready, 2)
                else:
                    pe.wait_ge(k_split, 2)
                for e in range(4):
                    b = 4 * n + e
                    last = mm(s_bank[n][:, C * e:C * e + C],
                              ct[:, b, :, :], wv[:, :], True, True)
                last.then_inc(v_mm, 1)
            pe.wait_ge(v_ready, 4)
            for k in range(4):
                scores_for_max(0, k, 0)
            max_transposed(0, 0)

            def step(i, turn):
                par, after = turn % 2, (turn + 1) % 4
                for k in range(2):
                    if has(i):
                        scores(i, k, turn)
                for k in range(2):
                    if has(i + 1):
                        scores_for_max(i + 1, k, after)
                if has(i + 2):
                    x_transposed(i + 2, par)
                if has(i):
                    scores(i, 2, turn)
                if has(i + 1):
                    scores_for_max(i + 1, 2, after)
                if has(i + 2):
                    project_q(i + 2)
                if has(i):
                    scores(i, 3, turn)
                if has(i + 1):
                    scores_for_max(i + 1, 3, after)
                if has(i - 1):
                    numerator(i - 1, 1 - par)
                if has(i + 2):
                    pe.wait_ge(qlo_done, i + 3)
                if has(i - 2):
                    project(i - 2, par)
                if has(i - 1):
                    denominator(i - 1, 1 - par, 0)
                if has(i - 2):
                    wait(pe, x1_done, i - 1)
                if has(i + 1):
                    max_transposed(i + 1, 1 - par)
                if has(i - 1):
                    denominator(i - 1, 1 - par, 1)

            steps(pe, step)

            def h_transposed(j, par):
                pe.wait_ge(h2_done, j + 1)
                wait(pe, hlo_done, j)
                for t in range(CH):
                    last = nc.tensor.transpose(od[:, P * t:P * t + P], h2[par][:, t, :], ident[:, :])
                last.then_inc(h2_tr, 1)

            pe.wait_ge(on_done, B)
            h_transposed(0, 0)

            def fc1(j, k, par):
                if k == 0:
                    pe.wait_ge(hlo_done, j + 1)
                wait(pe, gelu_done, KH * (j - 1) + k + 1)
                o = s_bank[k][:, :]
                mm(o, w1hl[:, 0, P * k:P * k + P], hhl[par][:, 0, :], True, False)
                mm(o, w1hl[:, 0, P * k:P * k + P], hhl[par][:, 1, :], False, False)
                mm(o, w1hl[:, 1, P * k:P * k + P], hhl[par][:, 0, :], False, True).then_inc(f1_mm, 1)

            def fc2(j, par):
                pe.wait_ge(gelu_done, KH * j + KH)
                wait(pe, y_done, j)
                for t in range(CH):
                    for k in range(KH):
                        last = mm(t_bank[par][:, C * t:C * t + C], gl[par][:, k, P * t:P * t + P],
                                  w[:, W2 + C * k:W2 + C * k + C], k == 0, k == KH - 1)
                last.then_inc(y_mm, 1)

            def mlp(j, par):
                for k in range(KH):
                    if hasc(j):
                        fc1(j, k, par)
                    if k == 1 and hasc(j + 1):
                        h_transposed(j + 1, 1 - par)
                if hasc(j - 1):
                    fc2(j - 1, 1 - par)

            chunk_steps(pe, mlp)


def bf16_bits(ones):
    return np.where(ones == 1, 0x3F80, 0).astype(np.uint16)


def constants():
    ident = np.eye(P, dtype=np.float32)
    hsel = np.zeros((P, HG), np.float32)
    for p in range(P):
        hsel[p, (p % R) // D] = 1
    vsel = np.zeros((P, 2, R), np.float32)
    for p in range(P):
        for a in range(2):
            h = 2 * a + p // M
            vsel[p, a, D * h:D * h + D] = 1
    rsel = np.zeros((MC, NPAIR, P), np.float32)
    for j in range(NPAIR):
        for e in range(2):
            for m in range(M):
                rsel[m, j, M * e + m] = 1
            for part in range(2):
                rsel[M + H * part + 2 * j + e, j, M * e:M * e + M] = 1
    return ident, bf16_bits(ident), hsel, vsel, bf16_bits(rsel)


def by_slot_row(w):
    return w.reshape(C, G, R).transpose(0, 2, 1).reshape(C, C)


def kernel(**inputs):
    import concourse.bacc as bacc
    from concourse.bass_utils import run_bass_kernel_spmd

    a = {k.replace("L0_xattn_", ""): np.asarray(v) for k, v in inputs.items()}
    mask = np.ascontiguousarray(a["mask_BxSxS2_bk0"].reshape(NT, P, M).transpose(1, 0, 2)).view(np.int32)
    fc2 = a["fc2_w"].reshape(KH, P, C).transpose(1, 0, 2).reshape(P, HID)
    weights = np.concatenate([by_slot_row(a["q_w"]), by_slot_row(a["kv_w"][:, :C]), a["kv_w"][:, C:], a["proj_w"],
                              a["fc1_w"], fc2], axis=1)
    vecs = np.stack([a["qn_w"], a["qn_b"], a["cn_w"], a["cn_b"], a["n2_w"], a["n2_b"],
                     *a["fc1_b"].reshape(KH, P)], axis=1)
    rows = np.stack([a["proj_b"], a["fc2_b"]])
    ident, identb, hsel, vsel, rsel = constants()
    arrays = {"x": a["x"], "ctx": a["ctx_1024"], "mask": mask, "weights": weights, "vecs": vecs, "rows": rows,
              "ident": ident, "identb": identb, "hsel": hsel, "vsel": vsel, "rsel": rsel}
    arrays = {k: np.ascontiguousarray(v) for k, v in arrays.items()}

    nc = bacc.Bacc("TRN2", target_bir_lowering=False, num_devices=1)
    aps = [nc.dram_tensor(f"in_{k}", v.shape, mybir.dt.from_np(v.dtype), kind="ExternalInput").ap()
           for k, v in arrays.items()]
    out = nc.dram_tensor("out", (B, N, C), F32, kind="ExternalOutput").ap()
    xattn_block(nc, *aps, out)
    r = run_bass_kernel_spmd(nc, [{f"in_{k}": v for k, v in arrays.items()}], core_ids=[0])
    return r.results[0]["out"]
```

```python
from contextlib import ExitStack

import numpy as np

import concourse.bass as bass
from concourse import mybir

F32 = mybir.dt.float32
F32R = mybir.dt.float32r
BF16 = mybir.dt.bfloat16
ALU = mybir.AluOpType
ACT = mybir.ActivationFunctionType
AX = mybir.AxisListType

P = 128
B, N, M, C = 16, 256, 64, 128
H = 16
D = C // H
HID = 4 * C
EPS = 1e-5
SCALE = float(D) ** -0.5
BIG = float(2.0 ** 96)
G = 4
HG = H // G
R = HG * D
TB = N // P
NT = B * TB
NC = B * M // P
XC = (0, 4, 16, NT)
NPAIR = H // 2
MC = M + 2 * H
KH = HID // P
CH = 4
NCH = NT // CH
NA = NT - 2 * CH
WQ, WK, WV, WP, W1, W2 = 0, C, 2 * C, 3 * C, 4 * C, 4 * C + HID
WCOLS = W2 + HID


def ds(start, size):
    return bass.ds(start, size)


def xattn_block(nc, x, ctx_in, mask, weights, vecs, rows, ident_in, identb_in, hsel_in, vsel_in,
                rsel_in, out):
    stack = ExitStack()
    with stack:
        def sb(name, shape, dt):
            return stack.enter_context(nc.sbuf_tensor(name, shape, dt))

        def sem(name):
            return stack.enter_context(nc.semaphore(name))

        bank = [stack.enter_context(nc.psum_tensor(f"bank{n}", [P, 512], F32)) for n in range(8)]

        w = sb("w", [P, WCOLS], F32)
        vec = sb("vec", [P, 6 + KH], F32)
        row = sb("row", [P, 2, C], F32)
        ident = sb("ident", [P, P], F32)
        identb = sb("identb", [P, P], BF16)
        hsel = sb("hsel", [P, HG], F32)
        vsel = sb("vsel", [P, 2, R], F32)
        rsel = sb("rsel", [MC, NPAIR, P], BF16)
        xs = sb("xs", [P, NT, C], F32)
        x1 = sb("x1", [P, NT, C], F32)
        wq = sb("wq", [P, C], F32)
        wk = sb("wk", [P, C], F32)
        wv = sb("wv", [P, C], F32)
        w1 = sb("w1", [P, HID], F32)
        w1hl = sb("w1hl", [P, 2, HID], F32R)
        b1 = sb("b1", [P, KH], F32)
        pb = sb("pb", [P, C], F32)
        fold = sb("fold", [P, 2, P], F32)
        fcol = sb("fcol", [P, 3], F32)
        ones = sb("ones", [P, P], F32)
        cs = sb("cs", [P, NC, C], F32)
        cn = sb("cn", [P, NC, C], F32)
        ct = sb("ct", [P, B, 2, M], F32)
        khl = sb("khl", [P, 2, B * M], F32R)
        ks = sb("ks", [P, G, B * M], F32R)
        vraw = sb("vraw", [P, B, C], F32)
        mkw = sb("mkw", [P, NT, M // 4], mybir.dt.int32)
        mk = mkw[:, :, :].bitcast(mybir.dt.uint8)
        maskbig = sb("maskbig", [P, NT, M], BF16)
        allm = sb("allm", [P, NT], F32)
        NS, N0 = NC + NT, NC + XC[1]
        stats = sb("stats", [P, NS, 6], F32)
        sa = sb("sa", [P, NS], F32)
        sd = sb("sd", [P, NS], F32)
        sq = sb("sq", [P, NS], F32)
        mean = sb("mean", [P, NS], F32)
        var = sb("var", [P, NS], F32)
        lnv = sb("lnv", [P, NS], F32)
        rseed = sb("rseed", [P, NS], F32)
        rstd = sb("rstd", [P, NS], F32)
        shift = sb("shift", [P, NS], F32)
        ln_done, nr_done, dr_done = sem("ln_done"), sem("nr_done"), sem("dr_done")
        stats2 = sb("stats2", [P, NT, 6], F32)
        xn = [sb(f"xn{p}", [P, TB, C], F32) for p in range(2)]
        xt = sb("xt", [P, N], F32)
        qhl = [sb(f"qhl{p}", [P, 2, N], F32R) for p in range(2)]
        qs = [sb(f"qs{p}", [P, G, N], F32R) for p in range(4)]
        kbd = [sb(f"kbd{p}", [P, G, HG, M], F32R) for p in range(2)]
        vbd = [sb(f"vbd{p}", [P, G, 2, R], F32) for p in range(2)]
        mc = [sb(f"mc{p}", [P, TB, MC], BF16) for p in range(2)]
        cmax = sb("cmax", [P, TB, H], F32)
        mct = [sb(f"mct{p}", [MC, N], BF16) for p in range(2)]
        pt = [sb(f"pt{p}", [P, NPAIR, N], F32) for p in range(2)]
        lnd = sb("lnd", [P, N], F32)
        rden = sb("rden", [P, N], F32)
        nr = sb("nr", [P, N], F32)
        dr = sb("dr", [P, N], F32)
        on = [sb(f"on{p}", [P, N], F32) for p in range(2)]
        h2 = [sb(f"h2{p}", [P, CH, C], F32) for p in range(2)]
        hhl = [sb(f"hhl{p}", [P, 2, CH * P], F32R) for p in range(2)]
        gl = [sb(f"gl{p}", [P, KH, CH * P], F32) for p in range(2)]
        x1b = [sb(f"x1b{p}", [P, CH, C], F32) for p in range(2)]
        yo = [sb(f"yo{p}", [P, CH, C], F32) for p in range(2)]

        s_bank = bank[0:4]
        t_bank = bank[4:6]
        od = bank[6]
        misc = bank[7]

        ld_w, ld_f, ld_v, ld_c, ld_k, ld_m = (
            sem("ld_w"), sem("ld_f"), sem("ld_v"), sem("ld_c"), sem("ld_k"), sem("ld_m"))
        ld_x = [sem(f"ld_x{n}") for n in range(3)]
        dve = sem("dve_chain")
        wfold_in, qfold_mm, wready, bfold_mm, b1_done, bv_copied, pb_mm = (
            sem("wfold_in"), sem("qfold_mm"), sem("wready"), sem("bfold_mm"), sem("b1_done"),
            sem("bv_copied"), sem("pb_mm"))
        var_ready, lnv_done, seed_ready, scales_ready = (
            sem("var_ready"), sem("lnv_done"), sem("seed_ready"), sem("scales_ready"))
        cn_ready, ct_tr, ct_ready, ct_twice, k_mm, k_hi, k_split = (
            sem("cn_ready"), sem("ct_tr"), sem("ct_ready"), sem("ct_twice"), sem("k_mm"), sem("k_hi"), sem("k_split"))
        ks_loaded = [sem(f"ks_loaded{n}") for n in range(2)]
        v_mm, v_ready, mask_ready, pb_ready = sem("v_mm"), sem("v_ready"), sem("mask_ready"), sem("pb_ready")
        w1_done, w1_hi, w1_split = sem("w1_done"), sem("w1_hi"), sem("w1_split")
        xn_done, xt_tr, xt_done, q_mm, qhi_done, qlo_done = (
            sem("xn_done"), sem("xt_tr"), sem("xt_done"), sem("q_mm"), sem("qhi_done"), sem("qlo_done"))
        qs_loaded = [sem(f"qs_loaded{p}") for p in range(4)]
        kbd_done, vbd_done, mcm_done, xb_done = sem("kbd_done"), sem("vbd_done"), sem("mcm_done"), sem("xb_done")
        s_mm, s_red, chi_done, clo_done, mct_tr, mct_done = (
            sem("s_mm"), sem("s_red"), sem("chi_done"), sem("clo_done"), sem("mct_tr"), sem("mct_done"))
        t_mm, exp_done, od_mm, rden_done, on_done, pj_mm, x1_done, st2_done = (
            sem("t_mm"), sem("exp_done"), sem("od_mm"), sem("rden_done"), sem("on_done"), sem("pj_mm"),
            sem("x1_done"), sem("st2_done"))
        h2_done, h2_tr, hhi_done, hlo_done, f1_mm, gelu_done, y_mm, y_done = (
            sem("h2_done"), sem("h2_tr"), sem("hhi_done"),
            sem("hlo_done"), sem("f1_mm"), sem("gelu_done"), sem("y_mm"), sem("y_done"))
        x1b_done = sem("x1b_done")
        yo_free = [sem("yo_free0"), sem("yo_free1")]

        block = stack.enter_context(nc.Block())

        def has(b):
            return not isinstance(b, int) or 0 <= b < B

        def hasc(j):
            return not isinstance(j, int) or 0 <= j < NCH

        def wait(eng, s, value):
            if not isinstance(value, int) or value > 0:
                eng.wait_ge(s, value)

        def value(eng, v):
            return v if isinstance(v, int) else eng.snap(v)

        def steps(eng, step):
            for i in range(2):
                step(i, i)
            with eng.Fori(0, (B - 4) // 4) as t:
                for e in range(2, 6):
                    step(4 * t + e, e % 4)
            step(B - 2, (B - 2) % 4)

        def copied_slots(b, turn):
            return 16 * (b - turn) + 64

        def chunk_steps(eng, step, first=0):
            for j in range(first, 2):
                step(j, j)
            with eng.Fori(0, 2) as t:
                step(2 * t + 2, 0)
                step(2 * t + 3, 1)
            for j in range(6, NCH + 1):
                step(j, j % 2)

        @block.sync
        def _(sp):
            for par in range(2):
                sp.sem_inc(yo_free[par], 16)
            xv = x.rearrange("b (t p) c -> p (b t) c", p=P)
            sp.dma_start(cs[:, :, :], ctx_in.rearrange("(u e) m c -> (e m) u c", e=2)).then_inc(ld_c, 16)
            sp.dma_start(xs[:, 0:XC[1], :], xv[:, 0:XC[1], :]).then_inc(ld_x[0], 16)
            sp.dma_start(vec[:, :], vecs).then_inc(ld_v, 16)
            sp.dma_start(ident[:, :], ident_in).then_inc(ld_v, 16)
            sp.dma_start(mkw[:, :, :], mask).then_inc(ld_k, 16)
            sp.dma_start(w[:, 0:W1], weights[:, 0:W1]).then_inc(ld_w, 16)
            sp.dma_start(xs[:, XC[1]:XC[2], :], xv[:, XC[1]:XC[2], :]).then_inc(ld_x[1], 16)
            sp.dma_start(w[:, W1:WCOLS], weights[:, W1:WCOLS]).then_inc(ld_f, 16)
            sp.dma_start(xs[:, XC[2]:XC[3], :], xv[:, XC[2]:XC[3], :]).then_inc(ld_x[2], 16)

            def key_slots(n):
                cols = slice(512 * n, 512 * n + 512)
                for part, done in enumerate((k_hi, k_split)):
                    sp.wait_ge(done, n + 1)
                    for s in (part, part + 2):
                        sp.dma_start(ks[R * s:R * s + R, :, cols].bitcast(F32), khl[:, part, cols].bitcast(F32))\
                          .then_inc(ks_loaded[n], 16)

            def slots(b, turn):
                for part, done in enumerate((qhi_done, qlo_done)):
                    sp.wait_ge(done, b + 1)
                    for s in range(2):
                        at = R * (2 * part + s)
                        sp.dma_start(qs[turn][at:at + R, :, :].bitcast(F32), qhl[turn % 2][:, part, :].bitcast(F32))\
                          .then_inc(qs_loaded[turn], 16)

            key_slots(0)
            slots(0, 0)
            slots(1, 1)
            key_slots(1)
            slots(2, 2)
            slots(3, 3)
            with sp.Fori(0, B // 4 - 1) as t:
                for e in range(4):
                    slots(4 * t + e + 4, e)

            ov = out.rearrange("b (t p) c -> p (b t) c", p=P)

            def store(j, par):
                first, ready = value(sp, CH * j), value(sp, j + 1)
                sp.wait_ge(y_done, ready)
                sp.dma_start(ov[:, ds(first, CH), :], yo[par][:, :, :]).then_inc(yo_free[par], 16)

            with sp.Fori(0, NCH // 2) as t:
                store(2 * t, 0)
                store(2 * t + 1, 1)
            for par in range(2):
                sp.wait_ge(yo_free[par], 16 * (NCH // 2) + 16)

        @block.gpsimd
        def _(pool):
            pool.dma_start(identb[:, :].bitcast(mybir.dt.uint16), identb_in).then_inc(ld_m, 16)
            pool.dma_start(row[:, :, :], rows.partition_broadcast(P)).then_inc(ld_m, 16)
            pool.dma_start(hsel[:, :], hsel_in).then_inc(ld_m, 16)
            pool.dma_start(vsel[:, :, :], vsel_in).then_inc(ld_m, 16)
            pool.dma_start(rsel[:, :, :].bitcast(mybir.dt.uint16), rsel_in).then_inc(ld_m, 16)
            pool.wait_ge(ld_f, 16)
            pool.wait_ge(ld_v, 32)
            nc.gpsimd.tensor_tensor(w1[:, :], w[:, W1:W1 + HID], vec[:, 4:5].to_broadcast([P, HID]), ALU.mult)\
                .then_inc(w1_done, 1)
            pool.wait_ge(ld_m, 80)
            pool.wait_ge(mask_ready, 1)

            def project_bias(b):
                nc.gpsimd.tensor_tensor(
                    x1[:, ds(TB * b, TB), :], xs[:, ds(TB * b, TB), :],
                    pb[:, :].unsqueeze(1).to_broadcast([P, TB, C]), ALU.add).then_inc(xb_done, 1)

            def prepare(b, par):
                wait(pool, mct_tr, b - 1)
                nc.gpsimd.tensor_copy(mc[par][:, :, 0:M], maskbig[:, ds(TB * b, TB), :]).then_inc(mcm_done, 1)
                if isinstance(b, int) and b == 0:
                    pool.wait_ge(ks_loaded[0], 64)
                wait(pool, t_mm, 4 * (b - 1))
                nc.gpsimd.tensor_tensor(
                    kbd[par][:, :, :, :],
                    ks[:, :, ds(M * b, M)].bitcast(F32).unsqueeze(2).to_broadcast([P, G, HG, M]),
                    hsel[:, :].unsqueeze(1).unsqueeze(3).to_broadcast([P, G, HG, M]), ALU.mult)\
                    .then_inc(kbd_done, 1)

            def prepare_v(b, par):
                wait(pool, od_mm, b - 1)
                nc.gpsimd.tensor_tensor(
                    vbd[par][:, :, :, :],
                    vraw[:, ds(b, 1), :].rearrange("p o (q r) -> p (o q) r", q=G).unsqueeze(2)
                    .to_broadcast([P, G, 2, R]),
                    vsel[:, :, :].unsqueeze(1).to_broadcast([P, G, 2, R]), ALU.mult).then_inc(vbd_done, 1)

            prepare(0, 0)
            prepare(1, 1)
            pool.wait_ge(w1_hi, 1)
            nc.gpsimd.tensor_tensor(w1hl[:, 1, :], w1[:, :], w1hl[:, 0, :].bitcast(F32), ALU.subtract)\
                .then_inc(w1_split, 1)
            pool.wait_ge(v_ready, 4)
            prepare_v(0, 0)
            pool.wait_ge(pb_ready, 1)
            for n in range(3):
                pool.wait_ge(ld_x[n], 16)
            project_bias(0)
            prepare(2, 0)
            prepare_v(1, 1)
            project_bias(1)
            pool.wait_ge(ks_loaded[1], 64)
            with pool.Fori(0, (B - 4) // 2) as t:
                prepare(2 * t + 3, 1)
                prepare_v(2 * t + 2, 0)
                project_bias(2 * t + 2)
                prepare(2 * t + 4, 0)
                prepare_v(2 * t + 3, 1)
                project_bias(2 * t + 3)
            prepare(B - 1, 1)
            prepare_v(B - 2, 0)
            project_bias(B - 2)
            prepare_v(B - 1, 1)
            project_bias(B - 1)

            def residual(j, par):
                pool.wait_ge(x1_done, B)
                wait(pool, y_done, j - 1)
                nc.gpsimd.tensor_tensor(
                    x1b[par][:, :, :], x1[:, ds(CH * j, CH), :],
                    row[:, 1:2, :].to_broadcast([P, CH, C]), ALU.add).then_inc(x1b_done, 1)

            residual(0, 0)
            residual(1, 1)
            with pool.Fori(0, NCH // 2 - 1) as t:
                residual(2 * t + 2, 0)
                residual(2 * t + 3, 1)

        @block.scalar
        def _(act):
            nc.scalar.preload_act_table_set("natural_log_exp_and_others")

            def seeds(turn, at, n):
                act.wait_ge(var_ready, turn + 1)
                nc.scalar.activation(lnv[:, at:at + n], var[:, at:at + n], ACT.Ln).then_inc(lnv_done, 1)
                act.wait_ge(lnv_done, turn + 1)
                nc.scalar.activation(rseed[:, at:at + n], lnv[:, at:at + n], ACT.Exp, scale=-0.5)\
                    .then_inc(seed_ready, 1)

            def context_copied(n, e, done):
                nc.scalar.activation(ct[:, 8 * n:8 * n + 8, e, :],
                                     t_bank[n][:, :].rearrange("p (b m) -> p b m", m=M), ACT.Copy).then_inc(done, 1)

            def k_high(n):
                act.wait_ge(k_mm, n + 1)
                nc.scalar.activation(khl[:, 0, 512 * n:512 * n + 512], s_bank[n][:, :], ACT.Identity,
                                     bias=fcol[:, 1:2]).then_inc(k_hi, 1)

            def normalise(b, par):
                wait(act, xt_tr, b - 1)
                for t in range(TB):
                    last = nc.scalar.activation(
                        xn[par][:, t, :], xs[:, ds(TB * b + t, 1), :].squeeze(1), ACT.Identity,
                        bias=shift[:, ds(NC + TB * b + t, 1)], scale=rstd[:, ds(NC + TB * b + t, 1)])
                last.then_inc(xn_done, 1)

            def x_copied(b):
                act.wait_ge(xt_tr, b + 1)
                nc.scalar.activation(xt[:, :], misc[:, 0:N], ACT.Copy).then_inc(xt_done, 1)

            def q_high(b, turn):
                act.wait_ge(q_mm, b + 1)
                if not isinstance(b, int) or b >= 2:
                    before = (turn + 2) % 4
                    act.wait_ge(qs_loaded[before], copied_slots(b - 2, before))
                nc.scalar.activation(qhl[turn % 2][:, 0, :], misc[:, 0:N], ACT.Copy).then_inc(qhi_done, 1)

            def inverse(b):
                act.wait_ge(od_mm, b + 1)
                nc.scalar.activation(lnd[:, :], od[:, N:2 * N], ACT.Ln).then_inc(ln_done, 1)
                act.wait_ge(ln_done, b + 1)
                nc.scalar.activation(rden[:, :], lnd[:, :], ACT.Exp, scale=-1.0).then_inc(rden_done, 1)

            def mct_copied(b, par):
                act.wait_ge(mct_tr, b + 1)
                nc.scalar.activation(mct[par][:, :], misc[0:MC, 0:N // 2].bitcast(BF16), ACT.Copy)\
                    .then_inc(mct_done, 1)

            seeds(0, 0, N0)
            act.wait_ge(ld_k, 16)
            nc.scalar.activation(maskbig[:, :, :], mk[:, :, :], ACT.Copy, scale=-BIG).then_inc(mask_ready, 1)
            for n in range(2):
                act.wait_ge(ct_tr, n + 1)
                context_copied(n, 0, ct_ready)
            act.wait_ge(scales_ready, 1)
            normalise(0, 0)
            act.wait_ge(wready, 4)
            k_high(0)
            x_copied(0)
            q_high(0, 0)
            k_high(1)
            normalise(1, 1)
            x_copied(1)
            q_high(1, 1)
            for n in range(2):
                context_copied(n, 1, ct_twice)
            act.wait_ge(w1_done, 1)
            nc.scalar.activation(w1hl[:, 0, :], w1[:, :], ACT.Copy).then_inc(w1_hi, 1)
            for n in range(4):
                if n == 1:
                    seeds(1, N0, NS - N0)
                act.wait_ge(v_mm, n + 1)
                nc.scalar.activation(vraw[:, 4 * n:4 * n + 4, :],
                                     t_bank[n % 2][:, :].rearrange("p (b c) -> p b c", c=C),
                                     ACT.Copy).then_inc(v_ready, 1)
            act.wait_ge(scales_ready, 2)

            def exps(b, k, par):
                if k == 0:
                    wait(act, od_mm, b - 1)
                act.wait_ge(t_mm, 4 * b + k + 1)
                nc.scalar.activation(pt[par][:, 2 * k:2 * k + 2, :],
                                     t_bank[k % 2][:, :].rearrange("p (j n) -> p j n", j=2),
                                     ACT.Exp, scale=SCALE).then_inc(exp_done, 1)

            def step(i, turn):
                par = turn % 2
                if has(i + 2):
                    normalise(i + 2, par)
                if has(i):
                    mct_copied(i, par)
                if has(i - 2):
                    inverse(i - 2)
                for k in range(4):
                    if has(i):
                        exps(i, k, par)
                    if k == 0 and has(i + 2):
                        x_copied(i + 2)
                    if k == 1 and has(i + 2):
                        q_high(i + 2, (turn + 2) % 4)

            steps(act, step)
            mct_copied(B - 1, 1)
            inverse(B - 3)
            seeds(2, 0, NA)

            def h_high(j, par):
                act.wait_ge(h2_tr, j + 1)
                wait(act, f1_mm, KH * (j - 1))
                nc.scalar.activation(hhl[par][:, 0, :], misc[:, :], ACT.Copy).then_inc(hhi_done, 1)

            inverse(B - 2)
            exps(B - 1, 0, 1)
            exps(B - 1, 1, 1)
            h_high(0, 0)
            exps(B - 1, 2, 1)
            exps(B - 1, 3, 1)
            inverse(B - 1)
            nc.scalar.preload_act_table_set("gelu_and_others")

            def mlp(j, par):
                for k in range(KH):
                    if hasc(j):
                        if k == 0:
                            wait(act, y_mm, j - 1)
                        act.wait_ge(f1_mm, KH * j + k + 1)
                        nc.scalar.activation(gl[par][:, k, :], s_bank[k][:, :], ACT.Gelu, bias=b1[:, k:k + 1])\
                            .then_inc(gelu_done, 1)
                    if k == 1 and hasc(j + 1):
                        h_high(j + 1, 1 - par)
                if isinstance(j, int) and j == 1:
                    nc.scalar.preload_act_table_set("natural_log_exp_and_others")
                    seeds(3, NA, NT - NA)
                    nc.scalar.preload_act_table_set("gelu_and_others")

            chunk_steps(act, mlp)

        @block.vector
        def _(v):
            chain = [0]

            def link(ins):
                chain[0] += 1
                ins.then_inc(dve, 1)
                v.wait_ge(dve, chain[0])

            def variance(st, at, n):
                c = slice(at, at + n)
                nc.vector.tensor_tensor(sa[:, c], st[:, c, 2], st[:, c, 5], ALU.add)
                nc.vector.tensor_tensor(mean[:, c], st[:, c, 1], st[:, c, 4], ALU.add)
                link(nc.vector.tensor_tensor(sd[:, c], st[:, c, 1], st[:, c, 4], ALU.subtract))
                nc.vector.tensor_scalar(mean[:, c], mean[:, c], 0.5, None, ALU.mult)
                nc.vector.tensor_scalar(sa[:, c], sa[:, c], 1.0 / C, EPS, ALU.mult, ALU.add)
                link(nc.vector.scalar_tensor_tensor(sq[:, c], sd[:, c], 0.25, sd[:, c], ALU.mult, ALU.mult))
                nc.vector.tensor_tensor(var[:, c], sq[:, c], sa[:, c], ALU.add).then_inc(var_ready, 1)

            def inverse_std(turn, at, n):
                c = slice(at, at + n)
                v.wait_ge(seed_ready, turn + 1)
                link(nc.vector.scalar_tensor_tensor(sa[:, c], var[:, c], -0.5, rseed[:, c], ALU.mult, ALU.mult))
                link(nc.vector.tensor_tensor(sq[:, c], sa[:, c], rseed[:, c], ALU.mult))
                link(nc.vector.scalar_tensor_tensor(rstd[:, c], sq[:, c], 1.5, rseed[:, c], ALU.add, ALU.mult))

            def all_masked(t0, t1):
                link(nc.vector.tensor_reduce(allm[:, t0:t1], mk[:, t0:t1, :], AX.X, ALU.min))
                link(nc.vector.tensor_scalar(allm[:, t0:t1], allm[:, t0:t1], -1.0, 1.0, ALU.mult, ALU.add))

            def x_scales(t0, t1):
                c = slice(NC + t0, NC + t1)
                link(nc.vector.tensor_tensor(rstd[:, c], rstd[:, c], allm[:, t0:t1], ALU.mult))
                link(nc.vector.tensor_tensor(shift[:, c], mean[:, c], rstd[:, c], ALU.mult))
                nc.vector.tensor_tensor(shift[:, c], allm[:, t0:t1], shift[:, c], ALU.subtract)\
                    .then_inc(scales_ready, 1)

            def x_stats(t0, t1):
                for t in range(t0, t1):
                    last = nc.vector.bn_stats(stats[:, NC + t, :], xs[:, t, :])
                return last

            nc.vector.memset(ones[:, :], 1.0)
            v.wait_ge(ld_c, 16)
            for u in range(NC):
                nc.vector.bn_stats(stats[:, u, :], cs[:, u, :])
            v.wait_ge(ld_x[0], 16)
            link(x_stats(0, XC[1]))
            variance(stats, 0, N0)
            v.wait_ge(ld_v, 32)
            link(nc.vector.tensor_tensor(fcol[:, 0:1], vec[:, 1:2], vec[:, 0:1], ALU.subtract))
            nc.vector.tensor_scalar(fold[:, 0, :], ones[:, :], fcol[:, 0:1], 1.0 / C, ALU.mult, ALU.mult)\
                .then_inc(wfold_in, 1)
            inverse_std(0, 0, N0)
            for u in range(NC):
                last = nc.vector.tensor_scalar(cn[:, u, :], cs[:, u, :], mean[:, u:u + 1], rstd[:, u:u + 1],
                                               ALU.subtract, ALU.mult)
                if u % 4 == 3:
                    last.then_inc(cn_ready, 1)
            v.wait_ge(ld_w, 16)
            nc.vector.tensor_scalar(wk[:, :], w[:, WK:WK + C], vec[:, 2:3], None, ALU.mult).then_inc(wready, 1)
            v.wait_ge(ld_k, 16)
            all_masked(0, XC[1])
            x_scales(0, XC[1])
            nc.vector.tensor_scalar(wv[:, :], w[:, WV:WV + C], vec[:, 2:3], None, ALU.mult).then_inc(wready, 1)
            v.wait_ge(qfold_mm, 1)
            nc.vector.scalar_tensor_tensor(wq[:, :], w[:, WQ:WQ + C], vec[:, 0:1], od[:, 128:128 + C],
                                           ALU.mult, ALU.add).then_inc(wready, 1)
            nc.vector.tensor_copy(fcol[:, 1:2], od[:, 0:1]).then_inc(wready, 1)
            nc.vector.tensor_scalar(fold[:, 1, :], ones[:, :], od[:, 1:2], None, ALU.mult).then_inc(bv_copied, 1)

            def k_low(n):
                v.wait_ge(k_hi, n + 1)
                nc.vector.scalar_tensor_tensor(
                    khl[:, 1, 512 * n:512 * n + 512], s_bank[n][:, :], fcol[:, 1:2],
                    khl[:, 0, 512 * n:512 * n + 512].bitcast(F32), ALU.add, ALU.subtract).then_inc(k_split, 1)

            def q_low(b, par):
                v.wait_ge(qhi_done, b + 1)
                nc.vector.tensor_tensor(qhl[par][:, 1, :], misc[:, 0:N], qhl[par][:, 0, :].bitcast(F32),
                                        ALU.subtract).then_inc(qlo_done, 1)

            def maxima(b, k):
                t, half = k // 2, k % 2
                v.wait_ge(s_mm, 4 * b + k + 1)
                nc.vector.tensor_reduce(cmax[:, t, 8 * half:8 * half + 8],
                                        s_bank[k][:, :].rearrange("p (h m) -> p h m", m=M), AX.X, ALU.max)\
                    .then_inc(s_red, 1)

            def max_parts(b, par):
                v.wait_ge(s_red, 4 * b + 4)
                wait(v, mct_tr, b - 1)
                nc.vector.tensor_scalar(mc[par][:, :, M:M + H], cmax[:, :, :], -1.0, None, ALU.mult)\
                    .then_inc(chi_done, 1)
                v.wait_ge(chi_done, b + 1)
                nc.vector.scalar_tensor_tensor(mc[par][:, :, M + H:MC], cmax[:, :, :], -1.0,
                                               mc[par][:, :, M:M + H], ALU.mult, ALU.subtract)\
                    .then_inc(clo_done, 1)

            def add_residual(b, pj=misc):
                v.wait_ge(pj_mm, b + 1)
                v.wait_ge(xb_done, b + 1)
                nc.vector.tensor_tensor(x1[:, ds(TB * b, TB), :], x1[:, ds(TB * b, TB), :],
                                        pj[:, 0:N].rearrange("p (t c) -> p t c", t=TB),
                                        ALU.subtract).then_inc(x1_done, 1)

            def quotient(b, par):
                v.wait_ge(rden_done, b + 1)
                nc.vector.tensor_tensor(nr[:, :], od[:, 0:N], rden[:, :], ALU.mult).then_inc(nr_done, 1)
                nc.vector.tensor_tensor(dr[:, :], od[:, N:2 * N], rden[:, :], ALU.mult).then_inc(dr_done, 1)
                v.wait_ge(nr_done, b + 1)
                v.wait_ge(dr_done, b + 1)
                nc.vector.scalar_tensor_tensor(on[par][:, :], dr[:, :], 2.0, nr[:, :], ALU.subtract, ALU.mult)\
                    .then_inc(on_done, 1)

            def row_stats(b):
                v.wait_ge(x1_done, b + 1)
                for t in range(TB):
                    last = nc.vector.bn_stats(stats2[:, ds(TB * b + t, 1), :].squeeze(1),
                                              x1[:, ds(TB * b + t, 1), :].squeeze(1))
                last.then_inc(st2_done, 1)

            v.wait_ge(ld_x[1], 16)
            x_stats(XC[1], 8)
            k_low(0)
            all_masked(XC[1], NT)
            q_low(0, 0)
            x_stats(8, XC[2])
            k_low(1)
            v.wait_ge(ld_m, 80)
            v.wait_ge(pb_mm, 1)
            nc.vector.tensor_tensor(pb[:, :], od[:, 0:C], row[:, 0, :], ALU.add).then_inc(pb_ready, 1)
            q_low(1, 1)
            v.wait_ge(ld_x[2], 16)
            link(x_stats(XC[2], NT))
            variance(stats, N0, NS - N0)
            v.wait_ge(bfold_mm, 1)
            nc.vector.tensor_tensor(b1[:, :], misc[:, 256:256 + KH], vec[:, 6:6 + KH], ALU.add).then_inc(b1_done, 1)
            for k in range(4):
                maxima(0, k)
            max_parts(0, 0)
            inverse_std(1, N0, NS - N0)
            x_scales(XC[1], NT)

            def step(i, turn):
                par = turn % 2
                for k in range(4):
                    if has(i + 1):
                        maxima(i + 1, k)
                    if k == 0 and has(i + 2):
                        q_low(i + 2, par)
                if has(i - 2):
                    add_residual(i - 2)
                if has(i + 1):
                    max_parts(i + 1, 1 - par)
                if has(i - 2):
                    row_stats(i - 2)
                if has(i - 1):
                    quotient(i - 1, 1 - par)

            steps(v, step)
            v.wait_ge(st2_done, B - 4)
            variance(stats2, 0, NA)

            def normalise(j, par):
                wait(v, h2_tr, j - 1)
                for t in range(CH):
                    last = nc.vector.tensor_scalar(
                        h2[par][:, t, :], x1[:, ds(CH * j + t, 1), :].squeeze(1), mean[:, ds(CH * j + t, 1)],
                        rstd[:, ds(CH * j + t, 1)], ALU.subtract, ALU.mult)
                last.then_inc(h2_done, 1)

            def h_low(j, par):
                v.wait_ge(hhi_done, j + 1)
                nc.vector.tensor_tensor(hhl[par][:, 1, :], misc[:, :], hhl[par][:, 0, :].bitcast(F32),
                                        ALU.subtract).then_inc(hlo_done, 1)

            def result(j, par):
                v.wait_ge(y_mm, j + 1)
                v.wait_ge(x1b_done, j + 1)
                v.wait_ge(yo_free[par], 16 * (j // 2 + 1) if isinstance(j, int) else 8 * (j - par) + 16)
                nc.vector.tensor_tensor(yo[par][:, :, :], t_bank[par][:, :].rearrange("p (t c) -> p t c", t=CH),
                                        x1b[par][:, :, :], ALU.add).then_inc(y_done, 1)

            add_residual(B - 3)
            inverse_std(2, 0, NA)
            normalise(0, 0)
            quotient(B - 2, 0)
            h_low(0, 0)
            normalise(1, 1)
            row_stats(B - 3)
            add_residual(B - 2, t_bank[0])
            row_stats(B - 2)
            quotient(B - 1, 1)

            def mlp(j, par):
                if hasc(j + 1):
                    h_low(j + 1, 1 - par)
                if isinstance(j, int) and j == 0:
                    add_residual(B - 1, t_bank[1])
                    row_stats(B - 1)
                    v.wait_ge(st2_done, B)
                    variance(stats2, NA, NT - NA)
                if hasc(j + 2):
                    normalise(j + 2, par)
                if hasc(j - 1):
                    result(j - 1, 1 - par)
                if isinstance(j, int) and j == 1:
                    inverse_std(3, NA, NT - NA)

            chunk_steps(v, mlp)

        @block.tensor
        def _(pe):
            def mm(o, lhsT, rhs, start, stop, **kw):
                return nc.tensor.matmul(o, lhsT, rhs, start=start, stop=stop, **kw)

            pe.wait_ge(ld_v, 32)
            pe.wait_ge(ld_w, 16)
            mm(od[:, 0:1], w[:, WK:WK + C], vec[:, 3:4], True, True)
            mm(od[:, 1:2], w[:, WV:WV + C], vec[:, 3:4], True, True)
            pe.wait_ge(wfold_in, 1)
            mm(od[:, 128:128 + C], fold[:, 0, :], w[:, WQ:WQ + C], True, True).then_inc(qfold_mm, 1)
            for n in range(2):
                pe.wait_ge(cn_ready, n + 1)
                for u in range(4):
                    last = nc.tensor.transpose(t_bank[n][:, P * u:P * u + P], cn[:, 4 * n + u, :], ident[:, :])
                last.then_inc(ct_tr, 1)

            def keys(n):
                pe.wait_ge(ct_ready, n + 1)
                mm(s_bank[n][:, :], wk[:, :], ct[:, 8 * n:8 * n + 8, 0, :], True, True).then_inc(k_mm, 1)

            def values(n):
                pe.wait_ge(ct_twice, 2)
                wait(pe, v_ready, n - 1)
                for e in range(4):
                    last = mm(t_bank[n % 2][:, C * e:C * e + C], ct[:, 4 * n + e, :, :], wv[:, :], True, True)
                last.then_inc(v_mm, 1)

            def x_transposed(b, par):
                pe.wait_ge(xn_done, b + 1)
                for t in range(TB):
                    last = nc.tensor.transpose(misc[:, P * t:P * t + P], xn[par][:, t, :], ident[:, :])
                last.then_inc(xt_tr, 1)

            def project_q(b):
                pe.wait_ge(xt_done, b + 1)
                mm(misc[:, 0:N], wq[:, :], xt[:, :], True, True).then_inc(q_mm, 1)

            def scores_for_max(b, k, turn):
                t, half, par = k // 2, k % 2, turn % 2
                if k == 0:
                    pe.wait_ge(kbd_done, b + 1)
                    pe.wait_ge(mcm_done, b + 1)
                    pe.wait_ge(qs_loaded[turn], copied_slots(b, turn))
                wait(pe, s_red, 4 * (b - 1) + k + 1)
                mm(s_bank[k][:, :], identb[:, :], mc[par][:, t, 0:M].unsqueeze(1).to_broadcast([P, 8, M]),
                   True, False)
                for e in range(2):
                    g = 2 * half + e
                    last = mm(s_bank[k][:, 256 * e:256 * e + 256], qs[turn][:, g, P * t:P * t + P],
                              kbd[par][:, g, :, :], False, e == 1)
                last.then_inc(s_mm, 1)

            def max_transposed(b, par):
                pe.wait_ge(clo_done, b + 1)
                for t in range(TB):
                    last = nc.tensor.transpose(misc[0:MC, 64 * t:64 * t + 64].bitcast(BF16), mc[par][:, t, :],
                                               identb[:, :])
                last.then_inc(mct_tr, 1)

            def scores(b, k, turn):
                par = turn % 2
                if k == 0:
                    pe.wait_ge(mct_done, b + 1)
                wait(pe, exp_done, 4 * b + k - 1)
                for a in range(2):
                    o = t_bank[k % 2][:, N * a:N * a + N]
                    mm(o, kbd[par][:, k, 2 * a:2 * a + 2, :], qs[turn][:, k, :], True, False)
                    last = mm(o, rsel[:, 2 * k + a, :], mct[par][:, :], False, True)
                last.then_inc(t_mm, 1)

            def weighted(par, lhs, off, a):
                for q in range(G):
                    last = mm(od[R * q:R * q + R, off:off + N], lhs(q, a), pt[par][:, 2 * q + a, :],
                              a == 0, a == 1, tile_position=(0, R * q))
                return last

            def numerator(b, par):
                pe.wait_ge(exp_done, 4 * b + 4)
                pe.wait_ge(vbd_done, b + 1)
                wait(pe, on_done, b)
                for a in range(2):
                    weighted(par, lambda q, a: vbd[par][:, q, a, :], 0, a)

            def denominator(b, par, a):
                last = weighted(par, lambda q, a: vsel[:, a, :], N, a)
                if a == 1:
                    last.then_inc(od_mm, 1)

            def project(b, par, pj=misc):
                pe.wait_ge(on_done, b + 1)
                for t in range(TB):
                    last = mm(pj[:, P * t:P * t + P], on[par][:, P * t:P * t + P], w[:, WP:WP + C], True, True)
                last.then_inc(pj_mm, 1)

            pe.wait_ge(wready, 1)
            keys(0)
            x_transposed(0, 0)
            keys(1)
            pe.wait_ge(wready, 4)
            project_q(0)
            pe.wait_ge(bv_copied, 1)
            mm(od[:, 0:C], fold[:, 1, :], w[:, WP:WP + C], True, True).then_inc(pb_mm, 1)
            pe.wait_ge(qlo_done, 1)
            x_transposed(1, 1)
            project_q(1)
            values(0)
            pe.wait_ge(qlo_done, 2)
            pe.wait_ge(ld_f, 16)
            for k in range(KH):
                last = mm(misc[:, 256 + k:257 + k], w[:, W1 + P * k:W1 + P * k + P], vec[:, 5:6], True, True)
            last.then_inc(bfold_mm, 1)
            pe.wait_ge(k_split, 2)
            for k in range(4):
                scores_for_max(0, k, 0)
            for n in range(1, 4):
                values(n)
            pe.wait_ge(b1_done, 1)
            max_transposed(0, 0)
            pe.wait_ge(v_ready, 4)

            def step(i, turn):
                par, after = turn % 2, (turn + 1) % 4
                for k in range(2):
                    if has(i):
                        scores(i, k, turn)
                if has(i + 2):
                    x_transposed(i + 2, par)
                for k in range(2):
                    if has(i + 1):
                        scores_for_max(i + 1, k, after)
                if has(i + 2):
                    project_q(i + 2)
                for k in range(2, 4):
                    if has(i):
                        scores(i, k, turn)
                    if has(i + 1):
                        scores_for_max(i + 1, k, after)
                if has(i + 2):
                    pe.wait_ge(qlo_done, i + 3)
                if has(i - 2):
                    project(i - 2, par)
                if has(i - 1):
                    numerator(i - 1, 1 - par)
                    denominator(i - 1, 1 - par, 0)
                if has(i - 2):
                    wait(pe, x1_done, i - 1)
                if has(i + 1):
                    max_transposed(i + 1, 1 - par)
                if has(i - 1):
                    denominator(i - 1, 1 - par, 1)

            steps(pe, step)

            def h_transposed(j, par):
                pe.wait_ge(h2_done, j + 1)
                wait(pe, hlo_done, j)
                for t in range(CH):
                    last = nc.tensor.transpose(misc[:, P * t:P * t + P], h2[par][:, t, :], ident[:, :])
                last.then_inc(h2_tr, 1)

            def fc1(j, k, par):
                if k == 0:
                    if isinstance(j, int) and j == 0:
                        pe.wait_ge(w1_split, 1)
                    pe.wait_ge(hlo_done, j + 1)
                wait(pe, gelu_done, KH * (j - 1) + k + 1)
                o = s_bank[k][:, :]
                mm(o, w1hl[:, 0, P * k:P * k + P], hhl[par][:, 0, :], True, False)
                mm(o, w1hl[:, 0, P * k:P * k + P], hhl[par][:, 1, :], False, False)
                mm(o, w1hl[:, 1, P * k:P * k + P], hhl[par][:, 0, :], False, True).then_inc(f1_mm, 1)

            def fc2(j, par):
                pe.wait_ge(gelu_done, KH * j + KH)
                if isinstance(j, int) and j == 0:
                    pe.wait_ge(x1_done, B)
                wait(pe, y_done, j)
                for t in range(CH):
                    for k in range(KH):
                        last = mm(t_bank[par][:, C * t:C * t + C], gl[par][:, k, P * t:P * t + P],
                                  w[:, W2 + C * k:W2 + C * k + C], k == 0, k == KH - 1)
                last.then_inc(y_mm, 1)

            def mlp(j, par):
                for k in range(KH):
                    if hasc(j):
                        fc1(j, k, par)
                    if k == 1 and hasc(j + 1):
                        h_transposed(j + 1, 1 - par)
                if hasc(j - 1):
                    fc2(j - 1, 1 - par)

            numerator(B - 2, 0)
            project(B - 3, 1)
            denominator(B - 2, 0, 0)
            denominator(B - 2, 0, 1)
            scores(B - 1, 0, 3)
            scores(B - 1, 1, 3)
            pe.wait_ge(x1_done, B - 2)
            h_transposed(0, 0)
            scores(B - 1, 2, 3)
            scores(B - 1, 3, 3)
            numerator(B - 1, 1)
            denominator(B - 1, 1, 0)
            denominator(B - 1, 1, 1)
            project(B - 2, 0, t_bank[0])
            for k in range(KH):
                fc1(0, k, 0)
            h_transposed(1, 1)
            project(B - 1, 1, t_bank[1])
            chunk_steps(pe, mlp, 1)


def bf16_bits(ones):
    return np.where(ones == 1, 0x3F80, 0).astype(np.uint16)


def constants():
    ident = np.eye(P, dtype=np.float32)
    hsel = np.zeros((P, HG), np.float32)
    for p in range(P):
        hsel[p, (p % R) // D] = 1
    vsel = np.zeros((P, 2, R), np.float32)
    for p in range(P):
        for a in range(2):
            h = 2 * a + p // M
            vsel[p, a, D * h:D * h + D] = 1
    rsel = np.zeros((MC, NPAIR, P), np.float32)
    for j in range(NPAIR):
        for e in range(2):
            for m in range(M):
                rsel[m, j, M * e + m] = 1
            for part in range(2):
                rsel[M + H * part + 2 * j + e, j, M * e:M * e + M] = 1
    return ident, bf16_bits(ident), hsel, vsel, bf16_bits(rsel)


def by_slot_row(w):
    return w.reshape(C, G, R).transpose(0, 2, 1).reshape(C, C)


def kernel(**inputs):
    import concourse.bacc as bacc
    from concourse.bass_utils import run_bass_kernel_spmd

    a = {k.replace("L0_xattn_", ""): np.asarray(v) for k, v in inputs.items()}
    mask = np.ascontiguousarray(a["mask_BxSxS2_bk0"].reshape(NT, P, M).transpose(1, 0, 2)).view(np.int32)
    fc2 = a["fc2_w"].reshape(KH, P, C).transpose(1, 0, 2).reshape(P, HID)
    weights = np.concatenate([by_slot_row(a["q_w"]), by_slot_row(a["kv_w"][:, :C]), a["kv_w"][:, C:], a["proj_w"],
                              a["fc1_w"], fc2], axis=1)
    vecs = np.stack([a["qn_w"], a["qn_b"], a["cn_w"], a["cn_b"], a["n2_w"], a["n2_b"],
                     *a["fc1_b"].reshape(KH, P)], axis=1)
    rows = np.stack([a["proj_b"], a["fc2_b"]])
    ident, identb, hsel, vsel, rsel = constants()
    arrays = {"x": a["x"], "ctx": a["ctx_1024"], "mask": mask, "weights": weights, "vecs": vecs, "rows": rows,
              "ident": ident, "identb": identb, "hsel": hsel, "vsel": vsel, "rsel": rsel}
    arrays = {k: np.ascontiguousarray(v) for k, v in arrays.items()}

    nc = bacc.Bacc("TRN2", target_bir_lowering=False, num_devices=1)
    aps = [nc.dram_tensor(f"in_{k}", v.shape, mybir.dt.from_np(v.dtype), kind="ExternalInput").ap()
           for k, v in arrays.items()]
    out = nc.dram_tensor("out", (B, N, C), F32, kind="ExternalOutput").ap()
    xattn_block(nc, *aps, out)
    r = run_bass_kernel_spmd(nc, [{f"in_{k}": v for k, v in arrays.items()}], core_ids=[0])
    return r.results[0]["out"]
```

```python
from contextlib import ExitStack

import numpy as np

import concourse.bass as bass
from concourse import mybir

F32 = mybir.dt.float32
F32R = mybir.dt.float32r
BF16 = mybir.dt.bfloat16
ALU = mybir.AluOpType
ACT = mybir.ActivationFunctionType
AX = mybir.AxisListType

P = 128
B, N, M, C = 16, 256, 64, 128
H = 16
D = C // H
HID = 4 * C
EPS = 1e-5
SCALE = float(D) ** -0.5
BIG = float(2.0 ** 96)
G = 4
HG = H // G
R = HG * D
TB = N // P
NT = B * TB
NC = B * M // P
XC = (0, 8, 16, NT)
NPAIR = H // 2
RX, RM = R, R + 2 * H
KH = HID // P
CH = 4
NCH = NT // CH
NA = NT - 2 * CH
WQ, WK, WV, WP, W1, W2 = 0, C, 2 * C, 3 * C, 4 * C, 4 * C + HID
WCOLS = W2 + HID


def ds(start, size):
    return bass.ds(start, size)


def xattn_block(nc, x, ctx_in, mask, mask_t, weights, vecs, rows, ident_in, identb_in, hsel_in, vsel_in,
                rsel_in, ident_m_in, out):
    stack = ExitStack()
    with stack:
        def sb(name, shape, dt):
            return stack.enter_context(nc.sbuf_tensor(name, shape, dt))

        def sem(name):
            return stack.enter_context(nc.semaphore(name))

        bank = [stack.enter_context(nc.psum_tensor(f"bank{n}", [P, 512], F32)) for n in range(8)]

        w = sb("w", [P, WCOLS], F32)
        vec = sb("vec", [P, 6 + KH], F32)
        row = sb("row", [P, 2, C], F32)
        ident = sb("ident", [P, P], F32)
        identb = sb("identb", [P, P], BF16)
        hsel = sb("hsel", [P, HG], F32)
        vsel = sb("vsel", [P, 2, R], F32)
        ident_m = sb("ident_m", [P, M], F32)
        rsel = sb("rsel", [P, NPAIR, P], F32R)
        xs = sb("xs", [P, NT, C], F32)
        x1 = sb("x1", [P, NT, C], F32)
        wq = sb("wq", [P, C], F32)
        wk = sb("wk", [P, C], F32)
        wv = sb("wv", [P, C], F32)
        w1 = sb("w1", [P, HID], F32)
        w1hl = sb("w1hl", [P, 2, HID], F32R)
        b1 = sb("b1", [P, KH], F32)
        pb = sb("pb", [P, C], F32)
        fold = sb("fold", [P, 2, P], F32)
        fcol = sb("fcol", [P, 3], F32)
        ones = sb("ones", [P, P], F32)
        cs = sb("cs", [P, NC, C], F32)
        cn = sb("cn", [P, NC, C], F32)
        ct = sb("ct", [P, B, 2, M], F32)
        khl = sb("khl", [P, 2, B * M], F32R)
        ks = sb("ks", [P, G, B * M], F32R)
        vraw = sb("vraw", [P, B, C], F32)
        mkw = sb("mkw", [P, NT, M // 4], mybir.dt.int32)
        mk = mkw[:, :, :].bitcast(mybir.dt.uint8)
        mktw = sb("mktw", [P, B // 2 * N // 4], mybir.dt.int32)
        mkt = mktw[:, :].bitcast(mybir.dt.uint8)
        maskt = sb("maskt", [P, B // 2, N], F32R)
        allm = sb("allm", [P, NT], F32)
        NS, N0 = NC + NT, NC + XC[1]
        stats = sb("stats", [P, NS, 6], F32)
        sa = sb("sa", [P, NS], F32)
        sd = sb("sd", [P, NS], F32)
        sq = sb("sq", [P, NS], F32)
        mean = sb("mean", [P, NS], F32)
        var = sb("var", [P, NS], F32)
        lnv = sb("lnv", [P, NS], F32)
        rseed = sb("rseed", [P, NS], F32)
        rstd = sb("rstd", [P, NS], F32)
        shift = sb("shift", [P, NS], F32)
        ln_done, nr_done, dr_done = sem("ln_done"), sem("nr_done"), sem("dr_done")
        stats2 = sb("stats2", [P, NT, 6], F32)
        xn = [sb(f"xn{p}", [P, TB, C], F32) for p in range(2)]
        xt = sb("xt", [P, N], F32)
        qhl = [sb(f"qhl{p}", [P, 2, N], F32R) for p in range(2)]
        qs = [sb(f"qs{p}", [P, G, N], F32R) for p in range(4)]
        kbd = [sb(f"kbd{p}", [P, G, HG, M], F32R) for p in range(2)]
        vbd = [sb(f"vbd{p}", [P, G, 2, R], F32) for p in range(2)]
        mc = [sb(f"mc{p}", [P, TB, P], BF16) for p in range(2)]
        qm = [sb(f"qm{p}", [P, G, N], F32R) for p in range(4)]
        km = [sb(f"km{p}", [P, G, HG, M], F32R) for p in range(2)]
        cmax = [sb(f"cmax{p}", [P, TB, H], F32) for p in range(2)]
        pt = [sb(f"pt{p}", [P, NPAIR, N], F32) for p in range(2)]
        lnd = sb("lnd", [P, N], F32)
        rden = sb("rden", [P, N], F32)
        nr = sb("nr", [P, N], F32)
        dr = sb("dr", [P, N], F32)
        on = [sb(f"on{p}", [P, N], F32) for p in range(2)]
        h2 = [sb(f"h2{p}", [P, CH, C], F32) for p in range(2)]
        hhl = [qs[p][:, :, :].rearrange("p (k a) n -> p k (a n)", k=2) for p in range(2)]
        gl = [pt[p][:, :, :].rearrange("p (k a) n -> p k (a n)", k=KH) for p in range(2)]
        x1b = [cs[:, CH * p:CH * p + CH, :] for p in range(2)]
        yo = [cn[:, CH * p:CH * p + CH, :] for p in range(2)]

        s_bank = bank[0:4]
        t_bank = bank[4:6]
        od = bank[6]
        misc = bank[7]

        ld_w, ld_f, ld_v, ld_c, ld_k, ld_t, ld_m = (
            sem("ld_w"), sem("ld_f"), sem("ld_v"), sem("ld_c"), sem("ld_k"), sem("ld_t"), sem("ld_m"))
        ld_x = [sem(f"ld_x{n}") for n in range(3)]
        dve = sem("dve_chain")
        wfold_in, qfold_mm, wready, bfold_mm, b1_done, bv_copied, pb_mm = (
            sem("wfold_in"), sem("qfold_mm"), sem("wready"), sem("bfold_mm"), sem("b1_done"),
            sem("bv_copied"), sem("pb_mm"))
        var_ready, lnv_done, seed_ready, scales_ready = (
            sem("var_ready"), sem("lnv_done"), sem("seed_ready"), sem("scales_ready"))
        cn_ready, ct_tr, ct_ready, ct_twice, k_mm, k_hi, k_split = (
            sem("cn_ready"), sem("ct_tr"), sem("ct_ready"), sem("ct_twice"), sem("k_mm"), sem("k_hi"), sem("k_split"))
        ks_loaded = [sem(f"ks_loaded{n}") for n in range(2)]
        v_mm, v_ready, mask_ready, pb_ready = sem("v_mm"), sem("v_ready"), sem("mask_ready"), sem("pb_ready")
        w1_done, w1_hi, w1_split = sem("w1_done"), sem("w1_hi"), sem("w1_split")
        xn_done, xt_tr, xt_done, q_mm, qhi_done, qlo_done = (
            sem("xn_done"), sem("xt_tr"), sem("xt_done"), sem("q_mm"), sem("qhi_done"), sem("qlo_done"))
        qs_loaded = [sem(f"qs_loaded{p}") for p in range(4)]
        qm_loaded = [sem(f"qm_loaded{p}") for p in range(4)]
        ld_i, ident_spread = sem("ld_i"), sem("ident_spread")
        zero_rsel, zero_km, ones_set = sem("zero_rsel"), sem("zero_km"), sem("ones_set")
        km_done, kbd_done, vbd_done, xb_done = sem("km_done"), sem("kbd_done"), sem("vbd_done"), sem("xb_done")
        s_mm, s_red, chi_done, clo_done, mct_tr, mct_done = (
            sem("s_mm"), sem("s_red"), sem("chi_done"), sem("clo_done"), sem("mct_tr"), sem("mct_done"))
        t_mm, exp_done, od_mm, rden_done, on_done, pj_mm, x1_done, st2_done = (
            sem("t_mm"), sem("exp_done"), sem("od_mm"), sem("rden_done"), sem("on_done"), sem("pj_mm"),
            sem("x1_done"), sem("st2_done"))
        h2_done, h2_tr, hhi_done, hlo_done, f1_mm, gelu_done, y_mm, y_done = (
            sem("h2_done"), sem("h2_tr"), sem("hhi_done"),
            sem("hlo_done"), sem("f1_mm"), sem("gelu_done"), sem("y_mm"), sem("y_done"))
        x1b_done, y_half = sem("x1b_done"), sem("y_half")
        yo_free = [sem("yo_free0"), sem("yo_free1")]

        block = stack.enter_context(nc.Block())

        def has(b):
            return not isinstance(b, int) or 0 <= b < B

        def hasc(j):
            return not isinstance(j, int) or 0 <= j < NCH

        def wait(eng, s, value):
            if not isinstance(value, int) or value > 0:
                eng.wait_ge(s, value)

        def value(eng, v):
            return v if isinstance(v, int) else eng.snap(v)

        def copy_mask(eng, b, turn):
            at, pair = M * (turn % 2), value(eng, (b - turn % 2) // 2)
            eng.dma_start(
                qm[turn][RM:P, :, :].bitcast(F32),
                maskt[at:at + M, ds(pair, 1), :].bitcast(F32).to_broadcast([M, G, N]))\
                .then_inc(qm_loaded[turn], 16)

        def steps(eng, step):
            for i in range(2):
                step(i, i)
            loops = (B - 5) // 4
            with eng.Fori(0, loops) as t:
                for e in range(2, 6):
                    step(4 * t + e, e % 4)
            for i in range(4 * loops + 2, B - 1):
                step(i, i % 4)

        def copied_slots(b, turn):
            return 16 * (b - turn) + 64

        def copied_for_max(b, turn):
            return 8 * (b - turn) + 48

        def chunk_steps(eng, step, first=0):
            for j in range(first, 2):
                step(j, j)
            with eng.Fori(0, 2) as t:
                step(2 * t + 2, 0)
                step(2 * t + 3, 1)
            for j in range(6, NCH + 1):
                step(j, j % 2)

        @block.sync
        def _(sp):
            for par in range(2):
                sp.sem_inc(yo_free[par], 16)
            xv = x.rearrange("b (t p) c -> p (b t) c", p=P)
            sp.dma_start(ident_m[RM:P, :], ident_m_in).then_inc(ld_i, 16)
            sp.dma_start(cs[:, :, :], ctx_in.rearrange("(u e) m c -> (e m) u c", e=2)).then_inc(ld_c, 16)
            sp.dma_start(xs[:, 0:XC[1], :], xv[:, 0:XC[1], :]).then_inc(ld_x[0], 16)
            sp.dma_start(vec[:, :], vecs).then_inc(ld_v, 16)
            sp.dma_start(ident[:, :], ident_in).then_inc(ld_v, 16)
            sp.dma_start(mkw[:, :, :], mask).then_inc(ld_k, 16)
            sp.dma_start(mktw[:, :], mask_t).then_inc(ld_t, 16)
            sp.dma_start(w[:, 0:W1], weights[:, 0:W1]).then_inc(ld_w, 16)
            sp.dma_start(xs[:, XC[1]:XC[2], :], xv[:, XC[1]:XC[2], :]).then_inc(ld_x[1], 16)
            sp.dma_start(w[:, W1:WCOLS], weights[:, W1:WCOLS]).then_inc(ld_f, 16)
            sp.dma_start(xs[:, XC[2]:XC[3], :], xv[:, XC[2]:XC[3], :]).then_inc(ld_x[2], 16)

            def key_slots(n):
                cols = slice(512 * n, 512 * n + 512)
                for part, done in enumerate((k_hi, k_split)):
                    sp.wait_ge(done, n + 1)
                    for s in (part, part + 2):
                        sp.dma_start(ks[R * s:R * s + R, :, cols].bitcast(F32), khl[:, part, cols].bitcast(F32))\
                          .then_inc(ks_loaded[n], 16)

            def slots(b, turn):
                for part, done in enumerate((qhi_done, qlo_done)):
                    sp.wait_ge(done, b + 1)
                    if part == 0:
                        sp.dma_start(qm[turn][0:R, :, :].bitcast(F32), qhl[turn % 2][:, 0, :].bitcast(F32))\
                          .then_inc(qm_loaded[turn], 16)
                    for s in range(2):
                        at = R * (2 * part + s)
                        sp.dma_start(qs[turn][at:at + R, :, :].bitcast(F32), qhl[turn % 2][:, part, :].bitcast(F32))\
                          .then_inc(qs_loaded[turn], 16)

            sp.wait_ge(zero_km, 2)

            def zero_place(turn):
                sp.dma_start(qm[turn][RX:RM, :, :].rearrange("p g n -> p (g n)").bitcast(F32),
                             km[0][RX:RM, :, :, :].rearrange("p g h m -> p (g h m)").bitcast(F32))\
                  .then_inc(qm_loaded[turn], 16)

            for b in range(2):
                zero_place(b)
            sp.wait_ge(mask_ready, 1)
            for b in range(2):
                copy_mask(sp, b, b)
            key_slots(0)
            for b in range(2, 4):
                zero_place(b)
            for b in range(2):
                slots(b, b)
            for b in range(2, 4):
                copy_mask(sp, b, b)
            slots(2, 2)
            key_slots(1)
            slots(3, 3)
            with sp.Fori(0, B // 4 - 1) as t:
                for e in range(4):
                    slots(4 * t + e + 4, e)

            ov = out.rearrange("b (t p) c -> p (b t) c", p=P)

            def store(j, par):
                first, ready = value(sp, CH * j), value(sp, j + 1)
                sp.wait_ge(y_done, ready)
                sp.dma_start(ov[:, ds(first, CH), :], yo[par][:, :, :]).then_inc(yo_free[par], 16)

            with sp.Fori(0, NCH // 2 - 1) as t:
                store(2 * t, 0)
                store(2 * t + 1, 1)
            store(NCH - 2, 0)
            for half in range(2):
                sp.wait_ge(y_done, NCH + half)
                t = CH // 2 * half
                sp.dma_start(ov[:, NT - CH + t:NT - CH + t + CH // 2, :], yo[1][:, t:t + CH // 2, :])\
                  .then_inc(yo_free[1], 16)
            sp.wait_ge(yo_free[0], 16 * (NCH // 2) + 16)
            sp.wait_ge(yo_free[1], 16 * (NCH // 2) + 32)

        @block.gpsimd
        def _(pool):
            pool.dma_start(identb[:, :].bitcast(mybir.dt.uint16), identb_in).then_inc(ld_m, 16)
            pool.dma_start(row[:, :, :], rows.partition_broadcast(P)).then_inc(ld_m, 16)
            pool.dma_start(hsel[:, :], hsel_in).then_inc(ld_m, 16)
            pool.dma_start(vsel[:, :, :], vsel_in).then_inc(ld_m, 16)
            pool.dma_start(rsel[RX:RM, :, :], rsel_in.bitcast(F32R)).then_inc(ld_m, 16)
            pool.wait_ge(ld_f, 16)
            pool.wait_ge(ld_v, 32)
            nc.gpsimd.tensor_tensor(w1[:, :], w[:, W1:W1 + HID], vec[:, 4:5].to_broadcast([P, HID]), ALU.mult)\
                .then_inc(w1_done, 1)
            pool.wait_ge(ld_m, 80)

            def project_bias(b):
                nc.gpsimd.tensor_tensor(
                    x1[:, ds(TB * b, TB), :], xs[:, ds(TB * b, TB), :],
                    pb[:, :].unsqueeze(1).to_broadcast([P, TB, C]), ALU.add).then_inc(xb_done, 1)

            def k_for_max(b, par):
                nc.gpsimd.tensor_tensor(
                    km[par][0:R, :, :, :],
                    ks[0:R, :, ds(M * b, M)].bitcast(F32).unsqueeze(2).to_broadcast([R, G, HG, M]),
                    hsel[0:R, :].unsqueeze(1).unsqueeze(3).to_broadcast([R, G, HG, M]), ALU.mult)\
                    .then_inc(km_done, 1)

            def k_slots(b, par):
                nc.gpsimd.tensor_tensor(
                    kbd[par][:, :, :, :],
                    ks[:, :, ds(M * b, M)].bitcast(F32).unsqueeze(2).to_broadcast([P, G, HG, M]),
                    hsel[:, :].unsqueeze(1).unsqueeze(3).to_broadcast([P, G, HG, M]), ALU.mult)\
                    .then_inc(kbd_done, 1)

            def prepare(b, par):
                pool.wait_ge(t_mm, 4 * (b - 1))
                if not isinstance(b, int) or b + 1 < B:
                    k_for_max(b + 1, 1 - par)
                k_slots(b, par)

            def prepare_v(b, par):
                wait(pool, od_mm, b - 1)
                nc.gpsimd.tensor_tensor(
                    vbd[par][:, :, :, :],
                    vraw[:, ds(b, 1), :].rearrange("p o (q r) -> p (o q) r", q=G).unsqueeze(2)
                    .to_broadcast([P, G, 2, R]),
                    vsel[:, :, :].unsqueeze(1).to_broadcast([P, G, 2, R]), ALU.mult).then_inc(vbd_done, 1)

            pool.wait_ge(ks_loaded[0], 64)
            k_for_max(0, 0)
            k_for_max(1, 1)
            k_slots(0, 0)
            pool.wait_ge(s_mm, 4)
            k_for_max(2, 0)
            k_slots(1, 1)
            pool.wait_ge(w1_hi, 1)
            nc.gpsimd.tensor_tensor(w1hl[:, 1, :], w1[:, :], w1hl[:, 0, :].bitcast(F32), ALU.subtract)\
                .then_inc(w1_split, 1)
            pool.wait_ge(v_ready, 4)
            prepare_v(0, 0)
            pool.wait_ge(pb_ready, 1)
            for n in range(3):
                pool.wait_ge(ld_x[n], 16)
            project_bias(0)
            prepare(2, 0)
            prepare_v(1, 1)
            project_bias(1)
            pool.wait_ge(ks_loaded[1], 64)
            with pool.Fori(0, (B - 4) // 2) as t:
                prepare(2 * t + 3, 1)
                prepare_v(2 * t + 2, 0)
                project_bias(2 * t + 2)
                prepare(2 * t + 4, 0)
                prepare_v(2 * t + 3, 1)
                project_bias(2 * t + 3)
            prepare(B - 1, 1)
            prepare_v(B - 2, 0)
            project_bias(B - 2)
            prepare_v(B - 1, 1)
            project_bias(B - 1)

            def residual(j, par):
                pool.wait_ge(x1_done, B)
                wait(pool, y_done, j - 1)
                nc.gpsimd.tensor_tensor(
                    x1b[par][:, :, :], x1[:, ds(CH * j, CH), :],
                    row[:, 1:2, :].to_broadcast([P, CH, C]), ALU.add).then_inc(x1b_done, 1)

            residual(0, 0)
            residual(1, 1)
            with pool.Fori(0, NCH // 2 - 1) as t:
                residual(2 * t + 2, 0)
                residual(2 * t + 3, 1)

        @block.scalar
        def _(act):
            nc.scalar.preload_act_table_set("natural_log_exp_and_others")

            act.wait_ge(ld_i, 16)
            for every in (km[0][RM:P, :, :, :].rearrange("p g h m -> p (g h) m"),
                          km[1][RM:P, :, :, :].rearrange("p g h m -> p (g h) m"),
                          rsel[RM:P, :, :].rearrange("p j (e m) -> p (j e) m", m=M)):
                last = nc.scalar.activation(every, ident_m[RM:P, :].unsqueeze(1).to_broadcast([M, H, M]), ACT.Copy)
            last.then_inc(ident_spread, 1)

            def seeds(turn, at, n):
                act.wait_ge(var_ready, turn + 1)
                nc.scalar.activation(lnv[:, at:at + n], var[:, at:at + n], ACT.Ln).then_inc(lnv_done, 1)
                act.wait_ge(lnv_done, turn + 1)
                nc.scalar.activation(rseed[:, at:at + n], lnv[:, at:at + n], ACT.Exp, scale=-0.5)\
                    .then_inc(seed_ready, 1)

            def context_copied(n, e, done):
                nc.scalar.activation(ct[:, 8 * n:8 * n + 8, e, :],
                                     t_bank[n][:, :].rearrange("p (b m) -> p b m", m=M), ACT.Copy).then_inc(done, 1)

            def k_high(n):
                act.wait_ge(k_mm, n + 1)
                nc.scalar.activation(khl[:, 0, 512 * n:512 * n + 512], s_bank[n][:, :], ACT.Identity,
                                     bias=fcol[:, 1:2]).then_inc(k_hi, 1)

            def normalise(b, par):
                wait(act, xt_tr, b - 1)
                for t in range(TB):
                    last = nc.scalar.activation(
                        xn[par][:, t, :], xs[:, ds(TB * b + t, 1), :].squeeze(1), ACT.Identity,
                        bias=shift[:, ds(NC + TB * b + t, 1)], scale=rstd[:, ds(NC + TB * b + t, 1)])
                last.then_inc(xn_done, 1)

            def x_copied(b):
                act.wait_ge(xt_tr, b + 1)
                nc.scalar.activation(xt[:, :], misc[:, 0:N], ACT.Copy).then_inc(xt_done, 1)

            def q_high(b, turn):
                act.wait_ge(q_mm, b + 1)
                if not isinstance(b, int) or b >= 2:
                    before = (turn + 2) % 4
                    act.wait_ge(qs_loaded[before], copied_slots(b - 2, before))
                nc.scalar.activation(qhl[turn % 2][:, 0, :], misc[:, 0:N], ACT.Copy).then_inc(qhi_done, 1)

            def inverse(b, nd=od):
                act.wait_ge(od_mm, b + 1)
                if isinstance(b, int) and b >= B - 2:
                    act.wait_ge(on_done, b)
                nc.scalar.activation(lnd[:, :], nd[:, N:2 * N], ACT.Ln).then_inc(ln_done, 1)
                act.wait_ge(ln_done, b + 1)
                nc.scalar.activation(rden[:, :], lnd[:, :], ACT.Exp, scale=-1.0).then_inc(rden_done, 1)

            def mct_copied(b, turn):
                act.wait_ge(mct_tr, b + 1)
                nc.scalar.activation(qm[turn][RX:RM, 0, :], misc[RX:RM, 0:N // 2].bitcast(BF16), ACT.Copy)\
                    .then_inc(mct_done, 1)

            def mask_copied(b, turn):
                copy_mask(act, b, turn)

            seeds(0, 0, NC)
            act.wait_ge(ld_t, 16)
            nc.scalar.activation(maskt[:, :, :], mkt.rearrange("p (b n) -> p b n", n=N), ACT.Copy, scale=-BIG)\
                .then_inc(mask_ready, 1)
            act.wait_ge(ct_tr, 1)
            context_copied(0, 0, ct_ready)
            seeds(1, NC, XC[1])
            act.wait_ge(wready, 3)
            k_high(0)
            act.wait_ge(ct_tr, 2)
            context_copied(1, 0, ct_ready)
            act.wait_ge(scales_ready, 1)
            normalise(0, 0)
            x_copied(0)
            q_high(0, 0)
            normalise(1, 1)
            k_high(1)
            x_copied(1)
            q_high(1, 1)
            for n in range(2):
                context_copied(n, 1, ct_twice)
            normalise(2, 0)

            def v_copied(n):
                act.wait_ge(v_mm, n + 1)
                nc.scalar.activation(vraw[:, 4 * n:4 * n + 4, :],
                                     t_bank[n % 2][:, :].rearrange("p (b c) -> p b c", c=C),
                                     ACT.Copy).then_inc(v_ready, 1)

            v_copied(0)
            x_copied(2)
            v_copied(1)
            q_high(2, 2)
            act.wait_ge(w1_done, 1)
            nc.scalar.activation(w1hl[:, 0, :], w1[:, :], ACT.Copy).then_inc(w1_hi, 1)
            v_copied(2)
            mct_copied(0, 0)
            normalise(3, 1)
            v_copied(3)

            def exps(b, k, par):
                if k == 0:
                    wait(act, od_mm, b - 1)
                act.wait_ge(t_mm, 4 * b + k + 1)
                nc.scalar.activation(pt[par][:, 2 * k:2 * k + 2, :],
                                     t_bank[k % 2][:, :].rearrange("p (j n) -> p j n", j=2),
                                     ACT.Exp, scale=SCALE).then_inc(exp_done, 1)

            def step(i, turn):
                par = turn % 2
                early = isinstance(i, int) and i == 0
                late = isinstance(i, int) and i == 1
                if has(i + 3) and not early and not late:
                    normalise(i + 3, 1 - par)
                    mask_copied(i + 3, (turn + 3) % 4)
                if has(i - 2):
                    inverse(i - 2)
                for k in range(4):
                    if has(i):
                        exps(i, k, par)
                    if k == 0 and has(i + 1):
                        mct_copied(i + 1, (turn + 1) % 4)
                    if k == 0 and late:
                        act.wait_ge(scales_ready, 2)
                        normalise(i + 3, 1 - par)
                        mask_copied(i + 3, (turn + 3) % 4)
                    if k == 1 and has(i + 3):
                        x_copied(i + 3)
                    if early and k == 2:
                        seeds(2, N0, NS - N0)
                    if k == (2 if early else 3) and has(i + 3):
                        q_high(i + 3, (turn + 3) % 4)
                    if k == 1 and isinstance(i, int) and i == B - 2:
                        seeds(3, 0, NA)

            steps(act, step)

            def h_high(j, par):
                act.wait_ge(h2_tr, j + 1)
                wait(act, f1_mm, KH * (j - 1))
                nc.scalar.activation(hhl[par][:, 0, :], misc[:, :], ACT.Copy).then_inc(hhi_done, 1)

            inverse(B - 3)
            exps(B - 1, 0, 1)
            exps(B - 1, 1, 1)
            h_high(0, 0)
            exps(B - 1, 2, 1)
            exps(B - 1, 3, 1)
            inverse(B - 2, s_bank[3])
            inverse(B - 1)
            nc.scalar.preload_act_table_set("gelu_and_others")

            def mlp(j, par):
                for k in range(KH):
                    if hasc(j):
                        if k == 0:
                            wait(act, y_mm, j - 1)
                        act.wait_ge(f1_mm, KH * j + k + 1)
                        nc.scalar.activation(gl[par][:, k, :], s_bank[k][:, :], ACT.Gelu, bias=b1[:, k:k + 1])\
                            .then_inc(gelu_done, 1)
                    if k == 1 and hasc(j + 1):
                        h_high(j + 1, 1 - par)
                if isinstance(j, int) and j == 1:
                    nc.scalar.preload_act_table_set("natural_log_exp_and_others")
                    seeds(4, NA, NT - NA)
                    nc.scalar.preload_act_table_set("gelu_and_others")

            chunk_steps(act, mlp)

        @block.vector
        def _(v):
            chain = [0]

            def link(ins):
                chain[0] += 1
                ins.then_inc(dve, 1)
                v.wait_ge(dve, chain[0])

            def variance(st, at, n):
                c = slice(at, at + n)
                nc.vector.tensor_tensor(sa[:, c], st[:, c, 2], st[:, c, 5], ALU.add)
                nc.vector.tensor_tensor(mean[:, c], st[:, c, 1], st[:, c, 4], ALU.add)
                link(nc.vector.tensor_tensor(sd[:, c], st[:, c, 1], st[:, c, 4], ALU.subtract))
                nc.vector.tensor_scalar(mean[:, c], mean[:, c], 0.5, None, ALU.mult)
                nc.vector.tensor_scalar(sa[:, c], sa[:, c], 1.0 / C, EPS, ALU.mult, ALU.add)
                link(nc.vector.scalar_tensor_tensor(sq[:, c], sd[:, c], 0.25, sd[:, c], ALU.mult, ALU.mult))
                nc.vector.tensor_tensor(var[:, c], sq[:, c], sa[:, c], ALU.add).then_inc(var_ready, 1)

            def inverse_std(turn, at, n):
                c = slice(at, at + n)
                v.wait_ge(seed_ready, turn + 1)
                link(nc.vector.scalar_tensor_tensor(sa[:, c], var[:, c], -0.5, rseed[:, c], ALU.mult, ALU.mult))
                link(nc.vector.tensor_tensor(sq[:, c], sa[:, c], rseed[:, c], ALU.mult))
                link(nc.vector.scalar_tensor_tensor(rstd[:, c], sq[:, c], 1.5, rseed[:, c], ALU.add, ALU.mult))

            def all_masked(t0, t1):
                link(nc.vector.tensor_reduce(allm[:, t0:t1], mk[:, t0:t1, :], AX.X, ALU.min))
                link(nc.vector.tensor_scalar(allm[:, t0:t1], allm[:, t0:t1], -1.0, 1.0, ALU.mult, ALU.add))

            def x_scales(t0, t1):
                c = slice(NC + t0, NC + t1)
                link(nc.vector.tensor_tensor(rstd[:, c], rstd[:, c], allm[:, t0:t1], ALU.mult))
                link(nc.vector.tensor_tensor(shift[:, c], mean[:, c], rstd[:, c], ALU.mult))
                nc.vector.tensor_tensor(shift[:, c], allm[:, t0:t1], shift[:, c], ALU.subtract)\
                    .then_inc(scales_ready, 1)

            def x_stats(t0, t1):
                for t in range(t0, t1):
                    last = nc.vector.bn_stats(stats[:, NC + t, :], xs[:, t, :])
                return last

            nc.vector.memset(ones[:, :], 1.0).then_inc(ones_set, 1)
            v.wait_ge(ones_set, 1)
            for par in range(2):
                nc.vector.tensor_scalar(km[par][RX:RM, :, :, :].rearrange("p g h m -> p (g h m)"),
                                        ones[RX:RM, 0:1].to_broadcast([2 * H, G * HG * M]), 0.0, None, ALU.mult)\
                    .then_inc(zero_km, 1)
            nc.vector.tensor_scalar(rsel[0:R, :, :], ones[0:R, :].unsqueeze(1).to_broadcast([R, NPAIR, P]), 0.0,
                                    None, ALU.mult).then_inc(zero_rsel, 1)
            for par in range(2):
                nc.vector.memset(mc[par][:, :, :], 0.0)
            v.wait_ge(ld_c, 16)
            for u in range(NC):
                last = nc.vector.bn_stats(stats[:, u, :], cs[:, u, :])
            link(last)
            variance(stats, 0, NC)
            v.wait_ge(ld_v, 32)
            link(nc.vector.tensor_tensor(fcol[:, 0:1], vec[:, 1:2], vec[:, 0:1], ALU.subtract))
            nc.vector.tensor_scalar(fold[:, 0, :], ones[:, :], fcol[:, 0:1], 1.0 / C, ALU.mult, ALU.mult)\
                .then_inc(wfold_in, 1)
            inverse_std(0, 0, NC)

            def context_normalised(n):
                for u in range(4 * n, 4 * n + 4):
                    last = nc.vector.tensor_scalar(cn[:, u, :], cs[:, u, :], mean[:, u:u + 1], rstd[:, u:u + 1],
                                                   ALU.subtract, ALU.mult)
                last.then_inc(cn_ready, 1)

            context_normalised(0)
            v.wait_ge(ld_w, 16)
            nc.vector.tensor_scalar(wk[:, :], w[:, WK:WK + C], vec[:, 2:3], None, ALU.mult).then_inc(wready, 1)
            v.wait_ge(ld_x[0], 16)
            link(x_stats(0, XC[1]))
            v.wait_ge(qfold_mm, 1)
            nc.vector.scalar_tensor_tensor(wq[:, :], w[:, WQ:WQ + C], vec[:, 0:1], od[:, 128:128 + C],
                                           ALU.mult, ALU.add).then_inc(wready, 1)
            nc.vector.tensor_copy(fcol[:, 1:2], od[:, 0:1]).then_inc(wready, 1)
            variance(stats, NC, XC[1])
            context_normalised(1)
            v.wait_ge(ld_k, 16)
            all_masked(0, XC[1])
            inverse_std(1, NC, XC[1])
            x_scales(0, XC[1])
            nc.vector.tensor_scalar(wv[:, :], w[:, WV:WV + C], vec[:, 2:3], None, ALU.mult).then_inc(wready, 1)
            nc.vector.tensor_scalar(fold[:, 1, :], ones[:, :], od[:, 1:2], None, ALU.mult).then_inc(bv_copied, 1)

            def k_low(n):
                v.wait_ge(k_hi, n + 1)
                nc.vector.scalar_tensor_tensor(
                    khl[:, 1, 512 * n:512 * n + 512], s_bank[n][:, :], fcol[:, 1:2],
                    khl[:, 0, 512 * n:512 * n + 512].bitcast(F32), ALU.add, ALU.subtract).then_inc(k_split, 1)

            def q_low(b, par):
                v.wait_ge(qhi_done, b + 1)
                nc.vector.tensor_tensor(qhl[par][:, 1, :], misc[:, 0:N], qhl[par][:, 0, :].bitcast(F32),
                                        ALU.subtract).then_inc(qlo_done, 1)

            def maxima(b, k, par):
                t, half = k // 2, k % 2
                v.wait_ge(s_mm, 4 * b + k + 1)
                nc.vector.tensor_reduce(cmax[par][:, t, 8 * half:8 * half + 8],
                                        s_bank[k][:, :].rearrange("p (h m) -> p h m", m=M), AX.X, ALU.max)\
                    .then_inc(s_red, 1)

            def max_parts(b, par):
                v.wait_ge(s_red, 4 * b + 4)
                wait(v, mct_tr, b - 1)
                nc.vector.tensor_scalar(mc[par][:, :, RX:RX + H], cmax[par][:, :, :], -1.0, None, ALU.mult)\
                    .then_inc(chi_done, 1)
                v.wait_ge(chi_done, b + 1)
                nc.vector.scalar_tensor_tensor(mc[par][:, :, RX + H:RM], cmax[par][:, :, :], -1.0,
                                               mc[par][:, :, RX:RX + H], ALU.mult, ALU.subtract)\
                    .then_inc(clo_done, 1)

            def add_residual(b, pj=misc):
                v.wait_ge(pj_mm, b + 1)
                v.wait_ge(xb_done, b + 1)
                nc.vector.tensor_tensor(x1[:, ds(TB * b, TB), :], x1[:, ds(TB * b, TB), :],
                                        pj[:, 0:N].rearrange("p (t c) -> p t c", t=TB),
                                        ALU.subtract).then_inc(x1_done, 1)

            def quotient(b, par, nd=od):
                v.wait_ge(rden_done, b + 1)
                nc.vector.tensor_tensor(nr[:, :], nd[:, 0:N], rden[:, :], ALU.mult).then_inc(nr_done, 1)
                nc.vector.tensor_tensor(dr[:, :], nd[:, N:2 * N], rden[:, :], ALU.mult).then_inc(dr_done, 1)
                v.wait_ge(nr_done, b + 1)
                v.wait_ge(dr_done, b + 1)
                nc.vector.scalar_tensor_tensor(on[par][:, :], dr[:, :], 2.0, nr[:, :], ALU.subtract, ALU.mult)\
                    .then_inc(on_done, 1)

            def row_stats(b):
                v.wait_ge(x1_done, b + 1)
                for t in range(TB):
                    last = nc.vector.bn_stats(stats2[:, ds(TB * b + t, 1), :].squeeze(1),
                                              x1[:, ds(TB * b + t, 1), :].squeeze(1))
                last.then_inc(st2_done, 1)

            k_low(0)
            v.wait_ge(ld_x[1], 16)
            x_stats(XC[1], 11)
            all_masked(XC[1], NT)
            q_low(0, 0)
            x_stats(11, XC[2])
            v.wait_ge(ld_x[2], 16)
            x_stats(XC[2], 18)
            k_low(1)
            x_stats(18, 24)
            q_low(1, 1)
            for k in range(4):
                maxima(0, k, 0)
            max_parts(0, 0)
            v.wait_ge(ld_m, 80)
            v.wait_ge(pb_mm, 1)
            nc.vector.tensor_tensor(pb[:, :], od[:, 0:C], row[:, 0, :], ALU.add).then_inc(pb_ready, 1)
            x_stats(24, 27)
            q_low(2, 0)
            x_stats(27, 28)
            for k in range(4):
                maxima(1, k, 1)
            max_parts(1, 1)

            link(x_stats(28, NT))
            variance(stats, N0, NS - N0)

            def late_start():
                inverse_std(2, N0, NS - N0)
                x_scales(XC[1], NT)

            def fc1_bias():
                v.wait_ge(bfold_mm, 1)
                nc.vector.tensor_tensor(b1[:, :], od[:, 0:KH], vec[:, 6:6 + KH], ALU.add).then_inc(b1_done, 1)

            def step(i, turn):
                par = turn % 2
                if isinstance(i, int) and i == B - 2:
                    v.wait_ge(st2_done, B - 4)
                    variance(stats2, 0, NA)
                if isinstance(i, int) and i == 1:
                    fc1_bias()
                if has(i - 2):
                    quotient(i - 2, par)
                for k in range(4):
                    if has(i + 2):
                        maxima(i + 2, k, par)
                    if k == 2 and has(i + 3):
                        q_low(i + 3, 1 - par)
                if has(i - 2):
                    add_residual(i - 2)
                if has(i + 2):
                    max_parts(i + 2, par)
                if has(i - 2):
                    row_stats(i - 2)
                if isinstance(i, int) and i == 0:
                    late_start()

            steps(v, step)

            def normalise(j, par):
                wait(v, h2_tr, j - 1)
                for t in range(CH):
                    last = nc.vector.tensor_scalar(
                        h2[par][:, t, :], x1[:, ds(CH * j + t, 1), :].squeeze(1), mean[:, ds(CH * j + t, 1)],
                        rstd[:, ds(CH * j + t, 1)], ALU.subtract, ALU.mult)
                last.then_inc(h2_done, 1)

            def h_low(j, par):
                v.wait_ge(hhi_done, j + 1)
                nc.vector.tensor_tensor(hhl[par][:, 1, :], misc[:, :], hhl[par][:, 0, :].bitcast(F32),
                                        ALU.subtract).then_inc(hlo_done, 1)

            def result(j, par):
                v.wait_ge(y_mm, j + 1)
                v.wait_ge(x1b_done, j + 1)
                v.wait_ge(yo_free[par], 16 * (j // 2 + 1) if isinstance(j, int) else 8 * (j - par) + 16)
                nc.vector.tensor_tensor(yo[par][:, :, :], t_bank[par][:, :].rearrange("p (t c) -> p t c", t=CH),
                                        x1b[par][:, :, :], ALU.add).then_inc(y_done, 1)

            def last_result(j, par):
                v.wait_ge(x1b_done, j + 1)
                v.wait_ge(yo_free[par], 16 * (j // 2 + 1))
                for half, (made, b) in enumerate(((y_half, t_bank[par]), (y_mm, od))):
                    v.wait_ge(made, 1 if half == 0 else j + 1)
                    t = slice(CH // 2 * half, CH // 2 * half + CH // 2)
                    nc.vector.tensor_tensor(yo[par][:, t, :], b[:, :].rearrange("p (t c) -> p t c", t=CH)[:, t, :],
                                            x1b[par][:, t, :], ALU.add).then_inc(y_done, 1)

            inverse_std(3, 0, NA)
            normalise(0, 0)
            quotient(B - 3, 1)
            h_low(0, 0)
            normalise(1, 1)
            add_residual(B - 3, s_bank[2])
            row_stats(B - 3)
            quotient(B - 2, 0, s_bank[3])
            quotient(B - 1, 1)
            add_residual(B - 2, t_bank[0])

            def mlp(j, par):
                if hasc(j + 1):
                    h_low(j + 1, 1 - par)
                if hasc(j + 2):
                    normalise(j + 2, par)
                if isinstance(j, int) and j == 0:
                    add_residual(B - 1, t_bank[1])
                    row_stats(B - 2)
                    row_stats(B - 1)
                    v.wait_ge(st2_done, B)
                    variance(stats2, NA, NT - NA)
                if isinstance(j, int) and j == NCH:
                    last_result(j - 1, 1 - par)
                elif hasc(j - 1):
                    result(j - 1, 1 - par)
                if isinstance(j, int) and j == 1:
                    inverse_std(4, NA, NT - NA)

            chunk_steps(v, mlp)

        @block.tensor
        def _(pe):
            def mm(o, lhsT, rhs, start, stop, **kw):
                return nc.tensor.matmul(o, lhsT, rhs, start=start, stop=stop, **kw)

            pe.wait_ge(ld_v, 32)
            pe.wait_ge(ld_w, 16)
            mm(od[:, 0:1], w[:, WK:WK + C], vec[:, 3:4], True, True)
            mm(od[:, 1:2], w[:, WV:WV + C], vec[:, 3:4], True, True)
            pe.wait_ge(wfold_in, 1)
            mm(od[:, 128:128 + C], fold[:, 0, :], w[:, WQ:WQ + C], True, True).then_inc(qfold_mm, 1)
            def context_transposed(n):
                pe.wait_ge(cn_ready, n + 1)
                for u in range(4):
                    last = nc.tensor.transpose(t_bank[n][:, P * u:P * u + P], cn[:, 4 * n + u, :], ident[:, :])
                last.then_inc(ct_tr, 1)

            def keys(n):
                pe.wait_ge(ct_ready, n + 1)
                mm(s_bank[n][:, :], wk[:, :], ct[:, 8 * n:8 * n + 8, 0, :], True, True).then_inc(k_mm, 1)

            def values(n):
                pe.wait_ge(ct_twice, 2)
                pe.wait_ge(wready, 4)
                wait(pe, v_ready, n - 1)
                for e in range(4):
                    last = mm(t_bank[n % 2][:, C * e:C * e + C], ct[:, 4 * n + e, :, :], wv[:, :], True, True)
                last.then_inc(v_mm, 1)

            def x_transposed(b, par):
                pe.wait_ge(xn_done, b + 1)
                for t in range(TB):
                    last = nc.tensor.transpose(misc[:, P * t:P * t + P], xn[par][:, t, :], ident[:, :])
                last.then_inc(xt_tr, 1)

            def project_q(b):
                pe.wait_ge(xt_done, b + 1)
                mm(misc[:, 0:N], wq[:, :], xt[:, :], True, True).then_inc(q_mm, 1)

            def scores_for_max(b, k, turn):
                t, half, par = k // 2, k % 2, turn % 2
                if k == 0:
                    pe.wait_ge(km_done, b + 1)
                    pe.wait_ge(qm_loaded[turn], copied_for_max(b, turn))
                wait(pe, s_red, 4 * (b - 1) + k + 1)
                for e in range(2):
                    g = 2 * half + e
                    last = mm(s_bank[k][:, 256 * e:256 * e + 256], qm[turn][:, g, P * t:P * t + P],
                              km[par][:, g, :, :], True, True)
                last.then_inc(s_mm, 1)

            def max_transposed(b, par):
                pe.wait_ge(clo_done, b + 1)
                for t in range(TB):
                    last = nc.tensor.transpose(misc[:, 64 * t:64 * t + 64].bitcast(BF16), mc[par][:, t, :],
                                               identb[:, :])
                last.then_inc(mct_tr, 1)

            def scores(b, k, turn):
                par = turn % 2
                if k == 0:
                    pe.wait_ge(kbd_done, b + 1)
                    pe.wait_ge(qs_loaded[turn], copied_slots(b, turn))
                    pe.wait_ge(mct_done, b + 1)
                if isinstance(b, int) and b == 0 and k < 2:
                    pe.wait_ge(v_ready, 3 + k)
                wait(pe, exp_done, 4 * b + k - 1)
                for a in range(2):
                    o = t_bank[k % 2][:, N * a:N * a + N]
                    mm(o, kbd[par][:, k, 2 * a:2 * a + 2, :], qs[turn][:, k, :], True, False)
                    last = mm(o, rsel[:, 2 * k + a, :], qm[turn][:, 0, :], False, True)
                last.then_inc(t_mm, 1)

            def weighted(nd, par, lhs, off, a):
                for q in range(G):
                    last = mm(nd[R * q:R * q + R, off:off + N], lhs(q, a), pt[par][:, 2 * q + a, :],
                              a == 0, a == 1, tile_position=(0, R * q))
                return last

            def numerator(b, par, nd=od, read=None):
                pe.wait_ge(exp_done, 4 * b + 4)
                pe.wait_ge(vbd_done, b + 1)
                wait(pe, on_done, b if read is None else read)
                if isinstance(b, int) and b == 0:
                    pe.wait_ge(b1_done, 1)
                for a in range(2):
                    weighted(nd, par, lambda q, a: vbd[par][:, q, a, :], 0, a)

            def denominator(b, par, a, nd=od):
                last = weighted(nd, par, lambda q, a: vsel[:, a, :], N, a)
                if a == 1:
                    last.then_inc(od_mm, 1)

            def project(b, par, pj=misc):
                pe.wait_ge(on_done, b + 1)
                for t in range(TB):
                    last = mm(pj[:, P * t:P * t + P], on[par][:, P * t:P * t + P], w[:, WP:WP + C], True, True)
                last.then_inc(pj_mm, 1)

            def fc1_biases():
                pe.wait_ge(pb_ready, 1)
                pe.wait_ge(ld_f, 16)
                for k in range(KH):
                    last = mm(od[:, k:k + 1], w[:, W1 + P * k:W1 + P * k + P], vec[:, 5:6], True, True)
                last.then_inc(bfold_mm, 1)

            context_transposed(0)
            pe.wait_ge(wready, 1)
            keys(0)
            context_transposed(1)
            x_transposed(0, 0)
            pe.wait_ge(wready, 2)
            project_q(0)
            keys(1)
            pe.wait_ge(bv_copied, 1)
            mm(od[:, 0:C], fold[:, 1, :], w[:, WP:WP + C], True, True).then_inc(pb_mm, 1)
            pe.wait_ge(qlo_done, 1)
            x_transposed(1, 1)
            project_q(1)
            pe.wait_ge(k_split, 2)
            pe.wait_ge(ident_spread, 1)
            pe.wait_ge(zero_km, 2)
            pe.wait_ge(zero_rsel, 1)
            for k in range(4):
                scores_for_max(0, k, 0)
            values(0)
            pe.wait_ge(qlo_done, 2)
            x_transposed(2, 0)
            values(1)
            project_q(2)
            values(2)
            for k in range(4):
                scores_for_max(1, k, 1)
            pe.wait_ge(qlo_done, 3)
            max_transposed(0, 0)
            values(3)

            def step(i, turn):
                par, ahead = turn % 2, (turn + 2) % 4
                for k in range(2):
                    if has(i):
                        scores(i, k, turn)
                if isinstance(i, int) and i == 1:
                    pe.wait_ge(qlo_done, 4)
                if has(i + 1):
                    max_transposed(i + 1, 1 - par)
                for k in range(2):
                    if has(i + 2):
                        scores_for_max(i + 2, k, ahead)
                if has(i):
                    scores(i, 2, turn)
                if has(i + 3):
                    pe.wait_ge(mct_done, i + 2)
                    x_transposed(i + 3, 1 - par)
                if has(i + 2):
                    scores_for_max(i + 2, 2, ahead)
                if has(i):
                    scores(i, 3, turn)
                if has(i + 3):
                    project_q(i + 3)
                if has(i + 2):
                    scores_for_max(i + 2, 3, ahead)
                if has(i - 1):
                    numerator(i - 1, 1 - par)
                    denominator(i - 1, 1 - par, 0)
                if isinstance(i, int) and i == 0:
                    fc1_biases()
                if has(i + 3) and not (isinstance(i, int) and i == 0):
                    pe.wait_ge(qlo_done, i + 4)
                if has(i - 2):
                    if isinstance(i, int):
                        pe.wait_ge(mct_done, min(i + 2, B))
                    project(i - 2, par)
                if has(i - 1):
                    denominator(i - 1, 1 - par, 1)
                if has(i - 2) and not has(i + 2):
                    pe.wait_ge(x1_done, i - 1)

            steps(pe, step)

            def h_transposed(j, par):
                pe.wait_ge(h2_done, j + 1)
                wait(pe, hlo_done, j)
                for t in range(CH):
                    last = nc.tensor.transpose(misc[:, P * t:P * t + P], h2[par][:, t, :], ident[:, :])
                last.then_inc(h2_tr, 1)

            def fc1(j, k, par):
                if isinstance(j, int) and j == 0:
                    if k == 0:
                        pe.wait_ge(w1_split, 1)
                    if k == 2:
                        pe.wait_ge(x1_done, B - 2)
                    if k == 3:
                        pe.wait_ge(on_done, B - 1)
                if k == 0:
                    pe.wait_ge(hlo_done, j + 1)
                wait(pe, gelu_done, KH * (j - 1) + k + 1)
                o = s_bank[k][:, :]
                mm(o, w1hl[:, 0, P * k:P * k + P], hhl[par][:, 0, :], True, False)
                mm(o, w1hl[:, 0, P * k:P * k + P], hhl[par][:, 1, :], False, False)
                mm(o, w1hl[:, 1, P * k:P * k + P], hhl[par][:, 0, :], False, True).then_inc(f1_mm, 1)

            def fc2(j, par):
                pe.wait_ge(gelu_done, KH * j + KH)
                if isinstance(j, int) and j == 0:
                    pe.wait_ge(x1_done, B)
                wait(pe, y_done, j)
                for t in range(CH):
                    halves = isinstance(j, int) and j == NCH - 1
                    o = od if halves and t >= CH // 2 else t_bank[par]
                    for k in range(KH):
                        last = mm(o[:, C * t:C * t + C], gl[par][:, k, P * t:P * t + P],
                                  w[:, W2 + C * k:W2 + C * k + C], k == 0, k == KH - 1)
                    if halves and t == CH // 2 - 1:
                        last.then_inc(y_half, 1)
                last.then_inc(y_mm, 1)

            def mlp(j, par):
                for k in range(KH):
                    if hasc(j):
                        fc1(j, k, par)
                    if k == 1 and hasc(j + 1):
                        h_transposed(j + 1, 1 - par)
                if hasc(j - 1):
                    fc2(j - 1, 1 - par)

            scores(B - 1, 0, 3)
            scores(B - 1, 1, 3)
            numerator(B - 2, 0, s_bank[3], 0)
            h_transposed(0, 0)
            scores(B - 1, 2, 3)
            scores(B - 1, 3, 3)
            denominator(B - 2, 0, 0, s_bank[3])
            denominator(B - 2, 0, 1, s_bank[3])
            project(B - 3, 1, s_bank[2])
            numerator(B - 1, 1, od, B - 2)
            denominator(B - 1, 1, 0)
            denominator(B - 1, 1, 1)
            fc1(0, 0, 0)
            project(B - 2, 0, t_bank[0])
            fc1(0, 1, 0)
            h_transposed(1, 1)
            fc1(0, 2, 0)
            fc1(0, 3, 0)
            project(B - 1, 1, t_bank[1])
            chunk_steps(pe, mlp, 1)


def bf16_bits(ones):
    return np.where(ones == 1, 0x3F80, 0).astype(np.uint16)


def constants():
    ident = np.eye(P, dtype=np.float32)
    hsel = np.zeros((P, HG), np.float32)
    for p in range(P):
        hsel[p, (p % R) // D] = 1
    vsel = np.zeros((P, 2, R), np.float32)
    for p in range(P):
        for a in range(2):
            h = 2 * a + p // M
            vsel[p, a, D * h:D * h + D] = 1
    rsel = np.zeros((2 * H, NPAIR, P), np.float32)
    for j in range(NPAIR):
        for e in range(2):
            for part in range(2):
                rsel[H * part + 2 * j + e, j, M * e:M * e + M] = 1
    return ident, bf16_bits(ident), hsel, vsel, rsel, np.eye(M, dtype=np.float32)


def by_slot_row(w):
    return w.reshape(C, G, R).transpose(0, 2, 1).reshape(C, C)


def kernel(**inputs):
    import concourse.bacc as bacc
    from concourse.bass_utils import run_bass_kernel_spmd

    a = {k.replace("L0_xattn_", ""): np.asarray(v) for k, v in inputs.items()}
    mask = np.ascontiguousarray(a["mask_BxSxS2_bk0"].reshape(NT, P, M).transpose(1, 0, 2)).view(np.int32)
    mask_t = np.ascontiguousarray(a["mask_BxSxS2_bk0"].reshape(B // 2, 2, N, M).transpose(1, 3, 0, 2)
                                  .reshape(P, B // 2 * N)).view(np.int32)
    fc2 = a["fc2_w"].reshape(KH, P, C).transpose(1, 0, 2).reshape(P, HID)
    weights = np.concatenate([by_slot_row(a["q_w"]), by_slot_row(a["kv_w"][:, :C]), a["kv_w"][:, C:], a["proj_w"],
                              a["fc1_w"], fc2], axis=1)
    vecs = np.stack([a["qn_w"], a["qn_b"], a["cn_w"], a["cn_b"], a["n2_w"], a["n2_b"],
                     *a["fc1_b"].reshape(KH, P)], axis=1)
    rows = np.stack([a["proj_b"], a["fc2_b"]])
    ident, identb, hsel, vsel, rsel, ident_m = constants()
    arrays = {"x": a["x"], "ctx": a["ctx_1024"], "mask": mask, "mask_t": mask_t, "weights": weights, "vecs": vecs, "rows": rows,
              "ident": ident, "identb": identb, "hsel": hsel, "vsel": vsel, "rsel": rsel,
              "ident_m": ident_m}
    arrays = {k: np.ascontiguousarray(v) for k, v in arrays.items()}

    nc = bacc.Bacc("TRN2", target_bir_lowering=False, num_devices=1)
    aps = [nc.dram_tensor(f"in_{k}", v.shape, mybir.dt.from_np(v.dtype), kind="ExternalInput").ap()
           for k, v in arrays.items()]
    out = nc.dram_tensor("out", (B, N, C), F32, kind="ExternalOutput").ap()
    xattn_block(nc, *aps, out)
    r = run_bass_kernel_spmd(nc, [{f"in_{k}": v for k, v in arrays.items()}], core_ids=[0])
    return r.results[0]["out"]
```
